# Optimizing a Trainium2 kernel written in Bass

```python
import numpy as np
import jax
import jax.numpy as jnp

def _softmax(x, axis=-1):
    return jax.nn.softmax(x, axis=axis)

def _gelu(x):
    return jax.nn.gelu(x, approximate=True)

def _silu(x):
    return jax.nn.silu(x)

def _sigmoid(x):
    return jax.nn.sigmoid(x)

def _layernorm(x, axis=-1, eps=1e-05):
    m = jnp.mean(x, axis=axis, keepdims=True)
    v = jnp.var(x, axis=axis, keepdims=True)
    return (x - m) / jnp.sqrt(v + eps)

def _scatter_add(tgt, idx, src, axis=0):
    return tgt.at[idx].add(src)

def _segment_sum(src, seg, n):
    return jax.ops.segment_sum(src, seg, n)
kernel_name = 'mk_adj_resnorm_d1_adj_r2_ba96ea'

def setup_inputs(seed: int=0):
    np.random.seed(seed)
    _w = jnp.asarray

    def _rec_inputs():
        import jax
        import jax.numpy as jnp
        _gk = jax.random.key(seed)
        x = 7.22e-05 + 1 * jax.random.normal(jax.random.fold_in(_gk, 1), (128, 64, 512), jnp.float32)
        _a = jax.random.bernoulli(jax.random.fold_in(_gk, 2), 0.0625, (64, 64))
        _a = jnp.logical_or(_a, jnp.eye(64, dtype=bool))
        _af = _a.astype(jnp.float32)
        adj = _af
        return (x, adj)
    x, adj = _rec_inputs()

    def _L0_gnn_setup():
        import jax, jax.numpy as jnp
        import numpy as np
        EPS = 1e-08

        def _row_stochastic_causal(A, causal_mask):
            A = A * causal_mask
            deg = jnp.maximum(A.sum(axis=-1, keepdims=True), EPS)
            return A / deg
        key = jax.random.key(seed)
        k = jax.random.split(key, 5)
        B, N, D = (4, 1024, 512)
        s = 1.0 / np.sqrt(D)
        h = jax.random.normal(k[0], (B, N, D), dtype=jnp.float32)
        W_lang = jax.random.normal(k[1], (D, D), dtype=jnp.float32) * s
        W_grav = jax.random.normal(k[2], (D, D), dtype=jnp.float32) * s
        W_V = jax.random.normal(k[3], (D, D), dtype=jnp.float32) * s
        W_O = jax.random.normal(k[4], (D, D), dtype=jnp.float32) * s
        causal_mask = jnp.tril(jnp.ones((N, N), dtype=jnp.float32))
        gate_logit = jnp.zeros((), jnp.float32)
        log_sigma = jnp.zeros((), jnp.float32)
        return {'h': h, 'causal_mask': causal_mask, 'W_lang': W_lang, 'W_grav': W_grav, 'W_V': W_V, 'W_O': W_O, 'gate_logit': gate_logit, 'log_sigma': log_sigma}
    _L0_gnn_all = _L0_gnn_setup()
    _L0_gnn_in = {k: v for k, v in _L0_gnn_all.items() if k in ('W_lang', 'W_grav', 'W_V', 'W_O', 'gate_logit', 'log_sigma')}
    del _L0_gnn_all
    return {'x': x, 'adj': adj, 'L0_gnn_W_lang': _L0_gnn_in['W_lang'], 'L0_gnn_W_grav': _L0_gnn_in['W_grav'], 'L0_gnn_W_V': _L0_gnn_in['W_V'], 'L0_gnn_W_O': _L0_gnn_in['W_O'], 'L0_gnn_gate_logit': _L0_gnn_in['gate_logit'], 'L0_gnn_log_sigma': _L0_gnn_in['log_sigma']}

def reference(x, adj, L0_gnn_W_lang, L0_gnn_W_grav, L0_gnn_W_V, L0_gnn_W_O, L0_gnn_gate_logit, L0_gnn_log_sigma):
    import jax
    import jax.numpy as jnp

    def _L0_gnn_ref(h, causal_mask, W_lang, W_grav, W_V, W_O, gate_logit, log_sigma):
        import jax, jax.numpy as jnp
        import numpy as np
        EPS = 1e-08

        def _row_stochastic_causal(A, causal_mask):
            A = A * causal_mask
            deg = jnp.maximum(A.sum(axis=-1, keepdims=True), EPS)
            return A / deg
        z_l = jnp.einsum('bnd,ed->bne', h, W_lang)
        z_g = jnp.einsum('bnd,ed->bne', h, W_grav)
        v = jnp.einsum('bnd,ed->bne', h, W_V)
        N = h.shape[-2]
        not_eye = 1.0 - jnp.eye(N, dtype=h.dtype)
        zn = z_l / jnp.maximum(jnp.linalg.norm(z_l, axis=-1, keepdims=True), EPS)
        A_l = jnp.maximum(jnp.einsum('bnd,bmd->bnm', zn, zn), 0.0) * not_eye
        sq = jnp.sum(z_g * z_g, axis=-1, keepdims=True)
        d2 = jnp.maximum(sq + jnp.swapaxes(sq, -1, -2) - 2.0 * jnp.einsum('bnd,bmd->bnm', z_g, z_g), 0.0)
        sigma = jnp.exp(log_sigma)
        A_g = jnp.exp(-d2 / (2.0 * sigma * sigma)) * not_eye
        K_l = _row_stochastic_causal(A_l, causal_mask)
        K_g = _row_stochastic_causal(A_g, causal_mask)
        w_l = jax.nn.sigmoid(gate_logit)
        K = w_l * K_l + (1.0 - w_l) * K_g
        out = jnp.einsum('bnm,bmd->bnd', K, v)
        return jnp.einsum('bnd,ed->bne', out, W_O)
    x = _layernorm(x + _L0_gnn_ref(x, adj, L0_gnn_W_lang, L0_gnn_W_grav, L0_gnn_W_V, L0_gnn_W_O, L0_gnn_gate_logit, L0_gnn_log_sigma), axis=-1)
    return x

_drawn_inputs = setup_inputs


def setup_inputs(seed=0):
    import zlib

    import numpy as np

    out = dict(_drawn_inputs(seed))
    spreads = {}
    factors = {}
    for name, (base, spread) in spreads.items():
        noise = np.random.default_rng([zlib.crc32(name.encode()), seed]).standard_normal(out[name].shape)
        drawn = base * np.exp(spread * noise) if base else spread * noise
        out[name] = jnp.asarray(drawn.astype(out[name].dtype))
    for name, factor in factors.items():
        out[name] = (out[name] * factor).astype(out[name].dtype)
    return out
```

```python
from contextlib import ExitStack

import concourse.bass as bass
from concourse import mybir
from concourse.alu_op_type import AluOpType as ALU

ACT = mybir.ActivationFunctionType
F32 = mybir.dt.float32
F32R = mybir.dt.float32r
AX_X = mybir.AxisListType.X

P = 128
EPS_DEG = 1e-8
EPS_LN = 1e-5
LANG, GRAV = 0, 1


def adj_resnorm(nc, x, adj, w_lang, w_grav, w_v, w_o, gate_logit, log_sigma, out):
    NGRAPH, N, D = x.shape
    DC = D // P
    TILES = 4
    ROWS = TILES * P
    GROUPS = NGRAPH * N // ROWS
    RING = 4
    ZJOBS, VJOBS, TJOBS, OJOBS = 2 * DC, TILES, DC, TILES
    JOBS = ZJOBS + VJOBS + TJOBS + OJOBS
    HI_JOBS = ZJOBS + VJOBS + TJOBS
    SETUP_JOBS = DC + 2 * DC + DC
    assert ROWS == 512 and P == 2 * N and D == 512 and JOBS % RING == 0 and SETUP_JOBS % RING == 0
    assert GROUPS % 2 == 0 and GROUPS >= 4

    x_rows = x.rearrange("(g t a) n d -> g t (a n) d", t=TILES, a=2)
    out_rows = out.rearrange("(g t a) n d -> g t (a n) d", t=TILES, a=2)

    AHEAD = SETUP_JOBS

    def first_job(g):
        return AHEAD + OJOBS if isinstance(g, int) and g == 0 else g * JOBS + AHEAD

    def first_hi(g):
        return g * HI_JOBS + (SETUP_JOBS + TJOBS)

    def xT_done_job(g):
        return AHEAD + TJOBS if isinstance(g, int) and g == 0 else g * JOBS + (AHEAD - 1)

    with ExitStack() as ctx:
        def sb(name, shape, dt=F32):
            return ctx.enter_context(nc.sbuf_tensor(name, shape, dt))

        def sem(name):
            return ctx.enter_context(nc.semaphore(name))

        ring = [ctx.enter_context(nc.psum_tensor(f"ring{i}", [P, 512], F32)) for i in range(RING)]
        gram = ctx.enter_context(nc.psum_tensor("gram", [P, TILES, 2, P], F32))
        small = ctx.enter_context(nc.psum_tensor("small", [P, TILES, 2, P], F32))

        ident = sb("ident", [P, P])
        mask = sb("mask", [P, P])
        scal = sb("scal", [P, 9])
        exponent_scale = sb("exponent_scale", [P, TILES])
        w_pair = sb("w_pair", [P, TILES, 2])
        minus_half = sb("minus_half", [P, TILES])
        minus_one = sb("minus_one", [P, TILES, 2])
        plus_half = sb("plus_half", [P, TILES])
        ln_eps = sb("ln_eps", [P, TILES])
        w_rows = [sb(f"w_rows{i}", [P, DC, D]) for i in range(4)]
        u_hi = sb("u_hi", [P, 2, DC, D], F32R)
        u_lo = sb("u_lo", [P, 2, DC, D], F32R)
        c_hi = sb("c_hi", [P, DC, D], F32R)
        c_lo = sb("c_lo", [P, DC, D], F32R)

        xs = [sb(f"x{i}", [P, TILES, D]) for i in range(2)]
        hT_hi = [sb(f"hT_hi{i}", [P, DC, ROWS], F32R) for i in range(2)]
        hT_lo = [sb(f"hT_lo{i}", [P, DC, ROWS], F32R) for i in range(2)]
        yT_hi = sb("yT_hi", [P, DC, 2, ROWS], F32R)
        yT_lo = sb("yT_lo", [P, DC, 2, ROWS], F32R)
        v_hi = sb("v_hi", [P, TILES, D], F32R)
        v_lo = sb("v_lo", [P, TILES, D], F32R)
        raw, sym = (w_rows[0][:, 2 * i:2 * i + 2, :].rearrange("p c (a w m) -> p (c a) w m", w=2, m=P)
                    for i in range(2))
        lang0, dist, expd, grav_s = (w_rows[1][:, i, :].rearrange("p (t m) -> p t m", m=P) for i in range(DC))
        norm2 = sb("norm2", [P, TILES, 2])
        cols = sb("cols", [P, TILES, 2])
        clamped = sb("clamped", [P, TILES])
        exp_bias = sb("exp_bias", [P, TILES])
        att = sb("att", [P, TILES, 2, P])
        rowsum = sb("rowsum", [P, TILES, 2])
        norm = sb("norm", [P, TILES])
        least_sum = sb("least_sum", [P, TILES, 2])
        deg = sb("deg", [P, TILES, 2])
        deg_r = sb("deg_r", [P, TILES, 2])
        factor = sb("factor", [P, TILES, 2])
        kmat = sb("kmat", [P, TILES, P])
        kT_hi = sb("kT_hi", [P, TILES, P], F32R)
        kT_lo = sb("kT_lo", [P, TILES, P], F32R)
        res = sb("res", [P, TILES, D])
        woT = res
        stats = sb("stats", [P, TILES, 6])
        moments = sb("moments", [P, TILES, 2])
        var_eps = sb("var_eps", [P, TILES])
        rstd = sb("rstd", [P, TILES])

        w_loaded = [sem(f"w_loaded{i}") for i in range(4)]
        small_loaded = sem("small_loaded")
        x_loaded = [sem(f"x_loaded{i}") for i in range(2)]
        out_stored = sem("out_stored")
        consts = sem("consts")
        scalars = sem("scalars")
        sigma_exp = sem("sigma_exp")
        ring_filled = sem("ring_filled")
        hi_written = sem("hi_written")
        ring_drained = sem("ring_drained")
        gram_filled = sem("gram_filled")
        raw_copied = sem("raw_copied")
        rawT_filled = sem("rawT_filled")
        sym_ready = sem("sym_ready")
        diag_ready = sem("diag_ready")
        clamp_ready = sem("clamp_ready")
        cols_ready = sem("cols_ready")
        norm_ready = sem("norm_ready")
        spread_filled = sem("spread_filled")
        lang0_ready = sem("lang0_ready")
        lang_ready = sem("lang_ready")
        dist_ready = sem("dist_ready")
        exp_ready = sem("exp_ready")
        grav_ready = sem("grav_ready")
        sums_ready = sem("sums_ready")
        factor_ready = sem("factor_ready")
        grav_scaled = sem("grav_scaled")
        k_ready = sem("k_ready")
        kT_filled = sem("kT_filled")
        kT_hi_ready = sem("kT_hi_ready")
        kT_lo_ready = sem("kT_lo_ready")
        stats_ready = sem("stats_ready")
        moments_ready = sem("moments_ready")
        var_ready = sem("var_ready")
        rstd_ready = sem("rstd_ready")
        out_ready = sem("out_ready")

        def over_tiles(a):
            return a[:, :].rearrange("p (t m) -> p t m", t=1).to_broadcast([P, TILES, P])

        def groups(eng, first, middle, last):
            first(0, 0)
            with eng.Fori(0, GROUPS // 2 - 1) as pair:
                middle(pair * 2 + 1, 1)
                middle(pair * 2 + 2, 0)
            last(GROUPS - 1, 1)

        block = ctx.enter_context(nc.Block())

        @block.sync
        def _(sp):
            sp.dma_start(w_rows[0][:, :, :], w_lang.rearrange("(c p) d -> p c d", p=P)).then_inc(w_loaded[0], 16)
            sp.dma_start(w_rows[1][:, :, :], w_grav.rearrange("(c p) d -> p c d", p=P)).then_inc(w_loaded[1], 16)
            for t in range(TILES):
                sp.dma_start(xs[0][:, t, :], x_rows[0, t]).then_inc(x_loaded[0], 16)
            sp.dma_start(w_rows[3][:, :, :], w_o.rearrange("(c p) d -> p c d", p=P)).then_inc(w_loaded[3], 16)
            sp.dma_start(w_rows[2][:, :, :], w_v.rearrange("(c p) d -> p c d", p=P)).then_inc(w_loaded[2], 16)
            for t in range(TILES):
                sp.dma_start(xs[1][:, t, :], x_rows[1, t]).then_inc(x_loaded[1], 16)

            def load(g, par):
                for t in range(TILES):
                    sp.wait_ge(ring_drained, first_job(g) + (ZJOBS + t + 1))
                    src = x_rows[bass.ds(g + 1, 1), t].rearrange("g p d -> (g p) d")
                    sp.dma_start(xs[1 - par][:, t, :], src).then_inc(x_loaded[1 - par], 16)

            def store(g):
                for t in range(TILES):
                    sp.wait_ge(out_ready, g * TILES + (t + 1))
                    dst = out_rows[bass.ds(g, 1), t].rearrange("g p d -> (g p) d")
                    sp.dma_start(dst, res[:, t, :]).then_inc(out_stored, 16)

            def turn(g, par):
                load(g, par)
                store(g - 1)

            groups(sp, lambda g, par: None, turn, lambda g, par: store(g - 1))
            store(GROUPS - 1)
            sp.wait_ge(out_stored, 16 * TILES * GROUPS)

        @block.gpsimd
        def _(pool):
            pool.memset(ident[:, :], 0.0).then_inc(consts, 1)
            pool.memset(mask[:, :], 0.0).then_inc(consts, 1)
            pool.memset(minus_half[:, :], -0.5).then_inc(consts, 1)
            pool.memset(minus_one[:, :, :], -1.0).then_inc(consts, 1)
            pool.memset(plus_half[:, :], 0.5).then_inc(consts, 1)
            pool.memset(ln_eps[:, :], EPS_LN).then_inc(consts, 1)
            pool.memset(least_sum[:, :, :], EPS_DEG).then_inc(consts, 1)
            pool.wait_ge(consts, 7)
            pool.affine_select(out=ident[:, :], in_=ident[:, :], compare_op=ALU.not_equal, fill=1.0,
                               base=0, pattern=[[-1, P]], channel_multiplier=1).then_inc(consts, 1)
            for a in range(2):
                pool.dma_start(mask[a * N:(a + 1) * N, a * N:(a + 1) * N], adj).then_inc(small_loaded, 16)
            pool.dma_start(scal[:, 0:1], gate_logit.partition_broadcast(P)).then_inc(small_loaded, 16)
            pool.dma_start(scal[:, 1:2], log_sigma.partition_broadcast(P)).then_inc(small_loaded, 16)
            pool.wait_ge(small_loaded, 64)
            pool.affine_select(out=mask[:, :], in_=mask[:, :], compare_op=ALU.not_equal, fill=0.0,
                               base=0, pattern=[[-1, P]], channel_multiplier=1).then_inc(consts, 1)
            pool.wait_ge(scalars, 8)

            def norms(g):
                pool.wait_ge(diag_ready, g * 8 + 8)
                pool.tensor_tensor(exp_bias[:, :], norm2[:, :, GRAV], exponent_scale[:, :],
                                   ALU.mult).then_inc(cols_ready, 1)
                pool.tensor_copy(cols[:, :, GRAV], norm2[:, :, GRAV]).then_inc(cols_ready, 1)
                pool.tensor_scalar(clamped[:, :], norm2[:, :, LANG], EPS_DEG * EPS_DEG, None,
                                   ALU.max).then_inc(clamp_ready, 1)
                pool.wait_ge(clamp_ready, g + 1)
                pool.tensor_tensor(cols[:, :, LANG], clamped[:, :], minus_half[:, :],
                                   ALU.pow).then_inc(cols_ready, 1)
                pool.tensor_tensor(norm[:, :], clamped[:, :], plus_half[:, :], ALU.pow).then_inc(norm_ready, 1)
                pool.wait_ge(norm_ready, g * 2 + 1)
                pool.tensor_tensor(least_sum[:, :, LANG], norm[:, :], least_sum[:, :, GRAV],
                                   ALU.mult).then_inc(norm_ready, 1)

            def factors(g):
                pool.wait_ge(sums_ready, g * 2 + 2)
                pool.tensor_tensor(deg_r[:, :, :], deg[:, :, :], minus_one[:, :, :],
                                   ALU.pow).then_inc(factor_ready, 1)
                pool.wait_ge(factor_ready, g * 2 + 1)
                pool.tensor_tensor(factor[:, :, :], deg_r[:, :, :], w_pair[:, :, :],
                                   ALU.mult).then_inc(factor_ready, 1)

            def deviations(g):
                pool.wait_ge(moments_ready, g * TILES + TILES)
                pool.tensor_tensor(var_eps[:, :], moments[:, :, 1], ln_eps[:, :], ALU.add).then_inc(var_ready, 1)
                pool.wait_ge(var_ready, g + 1)
                pool.tensor_tensor(rstd[:, :], var_eps[:, :], minus_half[:, :], ALU.pow).then_inc(rstd_ready, 1)

            def turn(g, par):
                factors(g - 1)
                norms(g)
                deviations(g - 1)

            groups(pool, lambda g, par: norms(g), turn, turn)
            factors(GROUPS - 1)
            deviations(GROUPS - 1)

        @block.tensor
        def _(pe):
            def take(job):
                if not (isinstance(job, int) and job < RING):
                    pe.wait_ge(ring_drained, job - (RING - 1))

            def split3(psum, pairs):
                n = 0
                for a_hi, a_lo, b_hi, b_lo in pairs:
                    for a, b in ((a_hi, b_hi), (a_hi, b_lo), (a_lo, b_hi)):
                        n += 1
                        last = pe.matmul(psum, a, b, start=(n == 1), stop=(n == 3 * len(pairs)))
                return last

            def set_up_u(job, which):
                pe.wait_ge(w_loaded[which], 16)
                w = w_rows[which]
                for i in range(DC):
                    take(job + i)
                    for e in range(DC):
                        last = pe.matmul(ring[(job + i) % RING][:, i * P:], w[:, e, i * P:(i + 1) * P],
                                         w[:, e, i * P:], start=(e == 0), stop=(e == DC - 1))
                    last.then_inc(ring_filled, 1)

            def set_up_c(job):
                pe.wait_ge(w_loaded[3], 16)
                for f in range(DC):
                    take(job + f)
                    for e in range(DC):
                        last = pe.transpose(ring[(job + f) % RING][:, e * P:(e + 1) * P],
                                            w_rows[3][:, e, f * P:(f + 1) * P], ident[:, :])
                    last.then_inc(ring_filled, 1)
                pe.wait_ge(w_loaded[2], 16)
                pe.wait_ge(ring_drained, job + DC)
                for i in range(DC):
                    take(job + DC + i)
                    for f in range(DC):
                        last = pe.matmul(ring[(job + i) % RING][:, :], w_rows[2][:, f, i * P:(i + 1) * P],
                                         woT[:, f, :], start=(f == 0), stop=(f == DC - 1))
                    last.then_inc(ring_filled, 1)

            def x_transposes(job, off, g, par):
                pe.wait_ge(x_loaded[par], g * (8 * TILES) + 8 * TILES * (2 - par))
                for c in range(DC):
                    take(job + (off + c))
                    for t in range(TILES):
                        last = pe.transpose(ring[(off + c) % RING][:, t * P:(t + 1) * P],
                                            xs[par][:, t, c * P:(c + 1) * P], ident[:, :])
                    last.then_inc(ring_filled, 1)

            def z_job(job, k, par):
                which, j = divmod(k, DC)
                take(job + k)
                pairs = []
                for i in range(j + 1):
                    pairs.append((u_hi[:, which, i, j * P:(j + 1) * P], u_lo[:, which, i, j * P:(j + 1) * P],
                                  hT_hi[par][:, i, :], hT_lo[par][:, i, :]))
                split3(ring[k % RING][:, :], pairs).then_inc(ring_filled, 1)

            def v_job(job, off, t, par):
                take(job + off)
                tile = slice(t * P, (t + 1) * P)
                split3(ring[off % RING][:, :],
                       [(hT_hi[par][:, c, tile], hT_lo[par][:, c, tile], c_hi[:, c, :], c_lo[:, c, :])
                        for c in range(DC)]).then_inc(ring_filled, 1)

            def grams(job, g, par):
                pe.wait_ge(ring_drained, job + ZJOBS)
                for t in range(TILES):
                    tile = slice(t * P, (t + 1) * P)
                    last = split3(gram[:, t, :, :],
                                  [(hT_hi[par][:, c, tile], hT_lo[par][:, c, tile],
                                    yT_hi[:, c, :, tile], yT_lo[:, c, :, tile]) for c in range(DC)])
                    if t % 2:
                        last.then_inc(gram_filled, 1)

            def raw_transposes(g):
                pe.wait_ge(raw_copied, g * 2 + 2)
                for t in range(TILES):
                    for w in range(2):
                        last = pe.transpose(small[:, t, w, :], raw[:, t, w, :], ident[:, :])
                last.then_inc(rawT_filled, 1)

            def spread(g):
                pe.wait_ge(cols_ready, g * 3 + 3)
                pe.wait_ge(sym_ready, g + 1)
                for t in range(TILES):
                    for w in range(2):
                        last = pe.transpose(small[:, t, w, :], cols[:, t, w:w + 1].to_broadcast([P, P]), ident[:, :])
                last.then_inc(spread_filled, 1)

            def k_transposes(g):
                pe.wait_ge(k_ready, g * TILES + TILES)
                for t in range(TILES):
                    last = pe.transpose(small[:, t // 2, t % 2, :], kmat[:, t, :], ident[:, :])
                last.then_inc(kT_filled, 1)

            def out_jobs(job, off, g):
                pe.wait_ge(kT_lo_ready, g + 1)
                for t in range(TILES):
                    take(job + (off + t))
                    split3(ring[(off + t) % RING][:, :],
                           [(kT_hi[:, t, :], kT_lo[:, t, :], v_hi[:, t, :], v_lo[:, t, :])]).then_inc(ring_filled, 1)

            def turn(g, par, post=True, ahead=True):
                job = first_job(g)
                pe.wait_ge(ring_drained, xT_done_job(g))
                for k in range(6):
                    z_job(job, k, par)
                if post:
                    k_transposes(g - 1)
                z_job(job, 6, par)
                z_job(job, 7, par)
                off = ZJOBS
                if post:
                    out_jobs(job, off, g - 1)
                    off += OJOBS
                grams(job, g, par)
                v_job(job, off, 0, par)
                raw_transposes(g)
                v_job(job, off + 1, 1, par)
                v_job(job, off + 2, 2, par)
                off += 3
                if ahead:
                    x_transposes(job, off, g + 1, 1 - par)
                    off += TJOBS
                spread(g)
                v_job(job, off, 3, par)

            pe.wait_ge(consts, 8)
            set_up_u(0, LANG)
            set_up_u(DC, GRAV)
            x_transposes(2 * DC, 0, 0, 0)
            set_up_c(2 * DC + TJOBS)
            groups(pe, lambda g, par: turn(g, par, post=False), turn, lambda g, par: turn(g, par, ahead=False))
            k_transposes(GROUPS - 1)
            out_jobs(GROUPS * JOBS + (AHEAD - TJOBS), 0, GROUPS - 1)

        @block.scalar
        def _(act):
            act.wait_ge(small_loaded, 64)
            act.activation(scal[:, 2:3], scal[:, 0:1], ACT.Exp, scale=-1.0).then_inc(sigma_exp, 1)
            act.activation(scal[:, 3:4], scal[:, 1:2], ACT.Exp).then_inc(sigma_exp, 1)

            def hi(job, dst, src, scale=1.0):
                act.wait_ge(ring_filled, job + 1)
                act.activation(dst, src, ACT.Copy, scale=scale).then_inc(hi_written, 1)

            def z_hi(job, k):
                which, j = divmod(k, DC)
                hi(job + k, yT_hi[:, j, which, :], ring[k % RING][:, :])

            def exps(g):
                act.wait_ge(dist_ready, g + 1)
                for t in range(TILES):
                    act.activation(expd[:, t, :], dist[:, t, :], ACT.Exp, bias=exp_bias[:, t:t + 1],
                                   scale=scal[:, 7:8]).then_inc(exp_ready, 1)

            def grav_scale(g):
                act.wait_ge(factor_ready, g * 2 + 2)
                act.wait_ge(grav_ready, g + 1)
                for t in range(TILES):
                    act.activation(grav_s[:, t, :], att[:, t, GRAV, :], ACT.Copy,
                                   scale=factor[:, t, GRAV:GRAV + 1]).then_inc(grav_scaled, 1)

            def kT_hi_part(g):
                act.wait_ge(kT_filled, g + 1)
                act.activation(kT_hi[:, :, :], small[:, 0:2, :, :].rearrange("p t w m -> p (t w) m"),
                               ACT.Copy).then_inc(kT_hi_ready, 1)

            def turn(g, par, post=True, ahead=True):
                job = first_job(g)
                z_hi(job, 0)
                z_hi(job, 1)
                if post:
                    exps(g - 1)
                z_hi(job, 2)
                z_hi(job, 3)
                if post:
                    grav_scale(g - 1)
                z_hi(job, 4)
                z_hi(job, 5)
                if post:
                    kT_hi_part(g - 1)
                z_hi(job, 6)
                z_hi(job, 7)
                off = ZJOBS + (OJOBS if post else 0)
                for b in range(2):
                    act.wait_ge(gram_filled, g * 2 + (b + 1))
                    act.activation(raw[:, 2 * b:2 * b + 2, :, :], gram[:, 2 * b:2 * b + 2, :, :],
                                   ACT.Copy).then_inc(raw_copied, 1)
                for t in range(3):
                    hi(job + (off + t), v_hi[:, t, :], ring[(off + t) % RING][:, :])
                off += 3
                if ahead:
                    for c in range(DC):
                        hi(job + (off + c), hT_hi[1 - par][:, c, :], ring[(off + c) % RING][:, :])
                    off += TJOBS
                hi(job + off, v_hi[:, 3, :], ring[off % RING][:, :])

            for which in range(2):
                for i in range(DC):
                    bank = ring[i % RING]
                    job = which * DC + i
                    act.wait_ge(ring_filled, job + 1)
                    a = act.activation(u_hi[:, which, i, i * P:(i + 1) * P], bank[:, i * P:(i + 1) * P],
                                       ACT.Copy, scale=0.5)
                    if i < DC - 1:
                        a = act.activation(u_hi[:, which, i, (i + 1) * P:], bank[:, (i + 1) * P:], ACT.Copy)
                    a.then_inc(hi_written, 1)
            for c in range(DC):
                hi(2 * DC + c, hT_hi[0][:, c, :], ring[c % RING][:, :])
            for f in range(DC):
                hi(3 * DC + f, woT[:, f, 0:D // 2], ring[f % RING][:, 0:D // 2])
            for i in range(DC):
                hi(4 * DC + i, c_hi[:, i, :], ring[i % RING][:, :])
            groups(act, lambda g, par: turn(g, par, post=False), turn, lambda g, par: turn(g, par, ahead=False))
            exps(GROUPS - 1)
            grav_scale(GROUPS - 1)
            kT_hi_part(GROUPS - 1)

        @block.vector
        def _(dve):
            def lo(count, dst, src, hi_part):
                dve.wait_ge(hi_written, count)
                dve.tensor_tensor(dst, src, hi_part.bitcast(F32), ALU.subtract).then_inc(ring_drained, 1)

            def z_lo(base, k):
                which, j = divmod(k, DC)
                lo(base + (k + 1), yT_lo[:, j, which, :], ring[k % RING][:, :], yT_hi[:, j, which, :])

            def symmetric(g):
                dve.wait_ge(diag_ready, g * 8 + 8)
                dve.wait_ge(rawT_filled, g + 1)
                dve.tensor_tensor(sym[:, :, :, :], small[:, :, :, :], raw[:, :, :, :],
                                  ALU.add).then_inc(sym_ready, 1)
                dve.wait_ge(sym_ready, g + 1)
                dve.scalar_tensor_tensor(out=lang0[:, :, :], in0=sym[:, :, LANG, :], scalar=0.0,
                                         in1=over_tiles(mask), op0=ALU.max, op1=ALU.mult).then_inc(lang0_ready, 1)

            def diagonals(g):
                dve.wait_ge(raw_copied, g * 2 + 2)
                for t in range(TILES):
                    for w in range(2):
                        dve.tensor_tensor_reduce(sym[:, t, w, :], raw[:, t, w, :], ident[:, :], 2.0, 0.0, ALU.mult,
                                                 ALU.add, norm2[:, t, w:w + 1]).then_inc(diag_ready, 1)

            def distances(g):
                dve.wait_ge(spread_filled, g + 1)
                dve.scalar_tensor_tensor(out=dist[:, :, :], in0=sym[:, :, GRAV, :], scalar=-2.0,
                                         in1=small[:, :, GRAV, :], op0=ALU.mult, op1=ALU.add).then_inc(dist_ready, 1)
                dve.wait_ge(lang0_ready, g + 1)
                dve.tensor_tensor(att[:, :, LANG, :], lang0[:, :, :], small[:, :, LANG, :],
                                  ALU.mult).then_inc(lang_ready, 1)

            def gravity(g):
                dve.wait_ge(exp_ready, g * TILES + TILES)
                dve.scalar_tensor_tensor(out=att[:, :, GRAV, :], in0=expd[:, :, :], scalar=1.0,
                                         in1=over_tiles(mask), op0=ALU.min, op1=ALU.mult).then_inc(grav_ready, 1)
                dve.wait_ge(grav_ready, g + 1)
                dve.wait_ge(lang_ready, g + 1)
                dve.tensor_reduce(rowsum[:, :, :], att[:, :, :, :], AX_X, ALU.add).then_inc(sums_ready, 1)
                dve.wait_ge(norm_ready, g * 2 + 2)
                dve.wait_ge(sums_ready, g * 2 + 1)
                dve.tensor_tensor(deg[:, :, :], rowsum[:, :, :], least_sum[:, :, :], ALU.max).then_inc(sums_ready, 1)

            def combine(g):
                dve.wait_ge(factor_ready, g * 2 + 2)
                dve.wait_ge(grav_scaled, g * TILES + TILES)
                for t in range(TILES):
                    dve.scalar_tensor_tensor(out=kmat[:, t, :], in0=att[:, t, LANG, :],
                                             scalar=factor[:, t, LANG:LANG + 1], in1=grav_s[:, t, :],
                                             op0=ALU.mult, op1=ALU.add).then_inc(k_ready, 1)

            def kT_lo_part(g):
                dve.wait_ge(kT_hi_ready, g + 1)
                dve.tensor_tensor(kT_lo[:, :, :], small[:, 0:2, :, :].rearrange("p t w m -> p (t w) m"),
                                  kT_hi[:, :, :].bitcast(F32), ALU.subtract).then_inc(kT_lo_ready, 1)

            def residual(job, off, g, par):
                if not isinstance(g, int) or g > 0:
                    dve.wait_ge(out_stored, g * (16 * TILES))
                for t in range(TILES):
                    dve.wait_ge(ring_filled, job + (off + t + 1))
                    dve.tensor_tensor(res[:, t, :], ring[(off + t) % RING][:, :], xs[par][:, t, :],
                                      ALU.add).then_inc(ring_drained, 1)
                for t in range(TILES):
                    dve.wait_ge(ring_drained, job + (off + t + 1))
                    dve.bn_stats(stats[:, t, :], res[:, t, :]).then_inc(stats_ready, 1)

            def aggregate():
                for t in range(TILES):
                    dve.bn_aggr(moments[:, t, :], stats[:, t, :]).then_inc(moments_ready, 1)

            def normalise(g):
                dve.wait_ge(rstd_ready, g + 1)
                for t in range(TILES):
                    dve.tensor_scalar(res[:, t, :], res[:, t, :], moments[:, t, 0:1], rstd[:, t:t + 1],
                                      ALU.subtract, ALU.mult).then_inc(out_ready, 1)

            def turn(g, par, post=True, ahead=True):
                job = first_job(g)
                base = first_hi(g)
                z_lo(base, 0)
                if post:
                    distances(g - 1)
                z_lo(base, 1)
                z_lo(base, 2)
                if post:
                    gravity(g - 1)
                z_lo(base, 3)
                if post:
                    combine(g - 1)
                z_lo(base, 4)
                z_lo(base, 5)
                if post:
                    kT_lo_part(g - 1)
                z_lo(base, 6)
                z_lo(base, 7)
                off = ZJOBS
                if post:
                    residual(job, off, g - 1, 1 - par)
                    off += OJOBS
                    dve.wait_ge(stats_ready, g * TILES)
                n = ZJOBS
                diagonals(g)
                if post:
                    aggregate()
                lo(base + (n + 1), v_lo[:, 0, :], ring[off % RING][:, :], v_hi[:, 0, :])
                symmetric(g)
                lo(base + (n + 2), v_lo[:, 1, :], ring[(off + 1) % RING][:, :], v_hi[:, 1, :])
                if post:
                    normalise(g - 1)
                lo(base + (n + 3), v_lo[:, 2, :], ring[(off + 2) % RING][:, :], v_hi[:, 2, :])
                off += 3
                n += 3
                if ahead:
                    for c in range(DC):
                        lo(base + (n + c + 1), hT_lo[1 - par][:, c, :], ring[(off + c) % RING][:, :],
                           hT_hi[1 - par][:, c, :])
                    off += TJOBS
                    n += TJOBS
                lo(base + (n + 1), v_lo[:, 3, :], ring[off % RING][:, :], v_hi[:, 3, :])

            dve.wait_ge(sigma_exp, 2)
            dve.tensor_scalar(scal[:, 4:5], scal[:, 2:3], 1.0, None, ALU.add).then_inc(scalars, 1)
            dve.tensor_tensor(scal[:, 6:7], scal[:, 3:4], scal[:, 3:4], ALU.mult).then_inc(scalars, 1)
            dve.wait_ge(scalars, 2)
            dve.reciprocal(scal[:, 5:6], scal[:, 4:5]).then_inc(scalars, 1)
            dve.reciprocal(scal[:, 8:9], scal[:, 6:7]).then_inc(scalars, 1)
            dve.wait_ge(scalars, 4)
            dve.tensor_scalar(scal[:, 7:8], scal[:, 8:9], -0.5, None, ALU.mult).then_inc(scalars, 1)
            dve.tensor_copy(w_pair[:, :, 0], scal[:, 5:6].to_broadcast([P, TILES])).then_inc(scalars, 1)
            dve.wait_ge(scalars, 6)
            dve.tensor_scalar(w_pair[:, :, 1], w_pair[:, :, 0], -1.0, 1.0, ALU.mult, ALU.add).then_inc(scalars, 1)
            dve.wait_ge(scalars, 7)
            dve.tensor_copy(exponent_scale[:, :], scal[:, 7:8].to_broadcast([P, TILES])).then_inc(scalars, 1)

            dve.wait_ge(consts, 9)
            for which in range(2):
                for i in range(DC):
                    bank = ring[i % RING]
                    dve.wait_ge(hi_written, which * DC + i + 1)
                    d = dve.scalar_tensor_tensor(
                        out=u_lo[:, which, i, i * P:(i + 1) * P], in0=bank[:, i * P:(i + 1) * P], scalar=0.5,
                        in1=u_hi[:, which, i, i * P:(i + 1) * P].bitcast(F32), op0=ALU.mult, op1=ALU.subtract)
                    if i < DC - 1:
                        d = dve.tensor_tensor(u_lo[:, which, i, (i + 1) * P:], bank[:, (i + 1) * P:],
                                              u_hi[:, which, i, (i + 1) * P:].bitcast(F32), ALU.subtract)
                    d.then_inc(ring_drained, 1)
            for c in range(DC):
                lo(2 * DC + c + 1, hT_lo[0][:, c, :], ring[c % RING][:, :], hT_hi[0][:, c, :])
            for f in range(DC):
                dve.wait_ge(hi_written, 3 * DC + f + 1)
                dve.tensor_copy(woT[:, f, D // 2:], ring[f % RING][:, D // 2:]).then_inc(ring_drained, 1)
            for i in range(DC):
                lo(4 * DC + i + 1, c_lo[:, i, :], ring[i % RING][:, :], c_hi[:, i, :])
            groups(dve, lambda g, par: turn(g, par, post=False), turn, lambda g, par: turn(g, par, ahead=False))
            distances(GROUPS - 1)
            gravity(GROUPS - 1)
            combine(GROUPS - 1)
            kT_lo_part(GROUPS - 1)
            residual(GROUPS * JOBS + (AHEAD - TJOBS), 0, GROUPS - 1, 1)
            dve.wait_ge(stats_ready, GROUPS * TILES)
            aggregate()
            normalise(GROUPS - 1)


_INS = ['x', 'adj', 'L0_gnn_W_lang', 'L0_gnn_W_grav', 'L0_gnn_W_V', 'L0_gnn_W_O',
        'L0_gnn_gate_logit', 'L0_gnn_log_sigma']


def kernel(**inputs):
    import numpy as _np
    import concourse.bacc as _bacc
    from concourse import mybir as _mybir
    from concourse.bass_utils import run_bass_kernel_spmd as _run

    nc = _bacc.Bacc("TRN2", target_bir_lowering=False, num_devices=1)
    arrays, args = {}, []
    for name in _INS:
        a = _np.ascontiguousarray(inputs[name])
        if a.ndim == 0:
            a = a.reshape(1)
        arrays[f"in_{name}_dram"] = a
        args.append(nc.dram_tensor(f"in_{name}_dram", a.shape, _mybir.dt.from_np(a.dtype), kind="ExternalInput").ap())
    shape = inputs["x"].shape
    args.append(nc.dram_tensor("out_0_dram", shape, _mybir.dt.float32, kind="ExternalOutput").ap())
    adj_resnorm(nc, *args)
    r = _run(nc, [arrays], core_ids=[0])
    return r.results[0]["out_0_dram"]
```

```python
from contextlib import ExitStack

import concourse.bass as bass
from concourse import mybir
from concourse.alu_op_type import AluOpType as ALU

ACT = mybir.ActivationFunctionType
F32 = mybir.dt.float32
F32R = mybir.dt.float32r
AX_X = mybir.AxisListType.X

P = 128
EPS_DEG = 1e-8
EPS_LN = 1e-5
LANG, GRAV = 0, 1


def adj_resnorm(nc, x, adj, w_lang, w_grav, w_v, w_o, gate_logit, log_sigma, out):
    NGRAPH, N, D = x.shape
    DC = D // P
    TILES = 4
    ROWS = TILES * P
    GROUPS = NGRAPH * N // ROWS
    RING = 4
    ZJOBS, VJOBS, TJOBS, OJOBS = 2 * DC, TILES, DC, TILES
    JOBS = ZJOBS + VJOBS + TJOBS + OJOBS
    HI_JOBS = ZJOBS + VJOBS + TJOBS
    U_JOB, WOT_JOB, XT0_JOB, C_JOB = 0, 2 * DC, 3 * DC, 3 * DC + TJOBS
    SETUP_JOBS = 2 * DC + DC + DC
    assert ROWS == 512 and P == 2 * N and D == 512 and JOBS % RING == 0 and SETUP_JOBS % RING == 0
    assert GROUPS % 2 == 0 and GROUPS >= 4

    x_rows = x.rearrange("(g t a) n d -> g t (a n) d", t=TILES, a=2)
    out_rows = out.rearrange("(g t a) n d -> g t (a n) d", t=TILES, a=2)

    AHEAD = SETUP_JOBS

    def first_job(g):
        return AHEAD + OJOBS if isinstance(g, int) and g == 0 else g * JOBS + AHEAD

    def first_hi(g):
        return g * HI_JOBS + (SETUP_JOBS + TJOBS)

    with ExitStack() as ctx:
        def sb(name, shape, dt=F32):
            return ctx.enter_context(nc.sbuf_tensor(name, shape, dt))

        def sem(name):
            return ctx.enter_context(nc.semaphore(name))

        ring = [ctx.enter_context(nc.psum_tensor(f"ring{i}", [P, 512], F32)) for i in range(RING)]
        gram = ctx.enter_context(nc.psum_tensor("gram", [P, TILES, 2, P], F32))
        small = ctx.enter_context(nc.psum_tensor("small", [P, TILES, 2, P], F32))

        u_banks = [[bank[:, :] for bank in ring],
                   [b[:, i:i + 2, :, :].rearrange("p t w m -> p (t w m)") for b in (gram, small) for i in (0, 2)]]

        ident = sb("ident", [P, P])
        mask = sb("mask", [P, P])
        scal = sb("scal", [P, 9])
        exponent_scale = sb("exponent_scale", [P, TILES])
        w_pair = sb("w_pair", [P, TILES, 2])
        minus_half = sb("minus_half", [P, TILES])
        plus_half = sb("plus_half", [P, TILES])
        ln_eps = sb("ln_eps", [P, TILES])
        w_rows = [sb(f"w_rows{i}", [P, DC, D]) for i in range(4)]
        u_hi = sb("u_hi", [P, 2, DC, D], F32R)
        u_lo = sb("u_lo", [P, 2, DC, D], F32R)
        c_hi = sb("c_hi", [P, DC, D], F32R)
        c_lo = sb("c_lo", [P, DC, D], F32R)

        xs = [sb(f"x{i}", [P, TILES, D]) for i in range(2)]
        hT_hi = [sb(f"hT_hi{i}", [P, DC, ROWS], F32R) for i in range(2)]
        hT_lo = [sb(f"hT_lo{i}", [P, DC, ROWS], F32R) for i in range(2)]
        yT_hi = sb("yT_hi", [P, DC, 2, ROWS], F32R)
        yT_lo = sb("yT_lo", [P, DC, 2, ROWS], F32R)
        v_hi = sb("v_hi", [P, TILES, D], F32R)
        v_lo = sb("v_lo", [P, TILES, D], F32R)
        w_hi = [yT_hi[:, :, i, :] for i in range(2)] + [v_hi[:, :, :]]
        w_lo = [yT_lo[:, :, i, :] for i in range(2)] + [v_lo[:, :, :]]
        woT_hi, woT_lo = hT_hi[1], hT_lo[1]
        raw, sym = (w_rows[0][:, 2 * i:2 * i + 2, :].rearrange("p c (a w m) -> p (c a) w m", w=2, m=P)
                    for i in range(2))
        lang0, dist, expd, grav_s = (w_rows[1][:, i, :].rearrange("p (t m) -> p t m", m=P) for i in range(DC))
        norm2 = sb("norm2", [P, TILES, 2])
        cols = sb("cols", [P, TILES, 2])
        clamped = sb("clamped", [P, TILES])
        exp_bias = sb("exp_bias", [P, TILES])
        att = sb("att", [P, TILES, 2, P])
        rowsum = sb("rowsum", [P, TILES, 2])
        norm = sb("norm", [P, TILES])
        least_sum = sb("least_sum", [P, TILES, 2])
        deg = sb("deg", [P, TILES, 2])
        deg_r = sb("deg_r", [P, TILES, 2])
        factor = sb("factor", [P, TILES, 2])
        kmat = sb("kmat", [P, TILES, P])
        kT_hi = sb("kT_hi", [P, TILES, P], F32R)
        kT_lo = sb("kT_lo", [P, TILES, P], F32R)
        res = sb("res", [P, TILES, D])
        stats = sb("stats", [P, TILES, 6])
        moments = sb("moments", [P, TILES, 2])
        var_eps = sb("var_eps", [P, TILES])
        rstd = sb("rstd", [P, TILES])

        w_loaded = [[sem(f"w_loaded{i}_{e}") for e in range(DC)] for i in range(2)]
        wv_loaded = sem("wv_loaded")
        wo_loaded = sem("wo_loaded")
        w_hi_ready = sem("w_hi_ready")
        w_lo_ready = sem("w_lo_ready")
        small_loaded = sem("small_loaded")
        x_loaded = [sem(f"x_loaded{i}") for i in range(2)]
        out_stored = sem("out_stored")
        consts = sem("consts")
        scalars = sem("scalars")
        sigma_exp = sem("sigma_exp")
        ring_filled = sem("ring_filled")
        hi_written = sem("hi_written")
        ring_drained = sem("ring_drained")
        gram_filled = sem("gram_filled")
        raw_copied = sem("raw_copied")
        rawT_filled = sem("rawT_filled")
        sym_ready = sem("sym_ready")
        diag_ready = sem("diag_ready")
        clamp_ready = sem("clamp_ready")
        cols_ready = sem("cols_ready")
        norm_ready = sem("norm_ready")
        spread_filled = sem("spread_filled")
        lang0_ready = sem("lang0_ready")
        lang_ready = sem("lang_ready")
        dist_ready = sem("dist_ready")
        exp_ready = sem("exp_ready")
        grav_ready = sem("grav_ready")
        sums_ready = sem("sums_ready")
        factor_ready = sem("factor_ready")
        grav_scaled = sem("grav_scaled")
        k_ready = sem("k_ready")
        kT_filled = sem("kT_filled")
        kT_hi_ready = sem("kT_hi_ready")
        kT_lo_ready = sem("kT_lo_ready")
        stats_ready = sem("stats_ready")
        moments_ready = sem("moments_ready")
        var_ready = sem("var_ready")
        rstd_ready = sem("rstd_ready")
        out_ready = sem("out_ready")

        def over_tiles(a):
            return a[:, :].rearrange("p (t m) -> p t m", t=1).to_broadcast([P, TILES, P])

        def groups(eng, first, middle, last):
            first(0, 0)
            with eng.Fori(0, GROUPS // 2 - 1) as pair:
                middle(pair * 2 + 1, 1)
                middle(pair * 2 + 2, 0)
            last(GROUPS - 1, 1)

        block = ctx.enter_context(nc.Block())

        @block.sync
        def _(sp):
            for which, w in enumerate((w_lang, w_grav)):
                for e in range(DC):
                    sp.dma_start(w_rows[which][:, e, :], w[e * P:(e + 1) * P, :]).then_inc(w_loaded[which][e], 16)
            for t in range(TILES):
                sp.dma_start(xs[0][:, t, :], x_rows[0, t]).then_inc(x_loaded[0], 16)
            sp.dma_start(w_rows[3][:, :, :], w_o.rearrange("(c p) d -> p c d", p=P)).then_inc(wo_loaded, 16)
            sp.dma_start(w_rows[2][:, :, :], w_v.rearrange("(c p) d -> p c d", p=P)).then_inc(wv_loaded, 16)
            for t in range(TILES):
                sp.dma_start(xs[1][:, t, :], x_rows[1, t]).then_inc(x_loaded[1], 16)

            def load(g, par):
                for t in range(TILES):
                    sp.wait_ge(ring_drained, first_job(g) + (ZJOBS + t + 1))
                    src = x_rows[bass.ds(g + 1, 1), t].rearrange("g p d -> (g p) d")
                    sp.dma_start(xs[1 - par][:, t, :], src).then_inc(x_loaded[1 - par], 16)

            def store(g):
                for t in range(TILES):
                    sp.wait_ge(out_ready, g * TILES + (t + 1))
                    dst = out_rows[bass.ds(g, 1), t].rearrange("g p d -> (g p) d")
                    sp.dma_start(dst, res[:, t, :]).then_inc(out_stored, 16)

            def turn(g, par):
                load(g, par)
                store(g - 1)

            groups(sp, lambda g, par: None, turn, lambda g, par: store(g - 1))
            store(GROUPS - 1)
            sp.wait_ge(out_stored, 16 * TILES * GROUPS)

        @block.gpsimd
        def _(pool):
            pool.memset(ident[:, :], 0.0).then_inc(consts, 1)
            pool.memset(mask[:, :], 0.0).then_inc(consts, 1)
            pool.memset(minus_half[:, :], -0.5).then_inc(consts, 1)
            pool.memset(plus_half[:, :], 0.5).then_inc(consts, 1)
            pool.memset(ln_eps[:, :], EPS_LN).then_inc(consts, 1)
            pool.memset(least_sum[:, :, :], EPS_DEG).then_inc(consts, 1)
            pool.wait_ge(consts, 6)
            pool.affine_select(out=ident[:, :], in_=ident[:, :], compare_op=ALU.not_equal, fill=1.0,
                               base=0, pattern=[[-1, P]], channel_multiplier=1).then_inc(consts, 1)
            for a in range(2):
                pool.dma_start(mask[a * N:(a + 1) * N, a * N:(a + 1) * N], adj).then_inc(small_loaded, 16)
            pool.dma_start(scal[:, 0:1], gate_logit.partition_broadcast(P)).then_inc(small_loaded, 16)
            pool.dma_start(scal[:, 1:2], log_sigma.partition_broadcast(P)).then_inc(small_loaded, 16)
            pool.wait_ge(small_loaded, 64)
            pool.affine_select(out=mask[:, :], in_=mask[:, :], compare_op=ALU.not_equal, fill=0.0,
                               base=0, pattern=[[-1, P]], channel_multiplier=1).then_inc(consts, 1)
            pool.wait_ge(scalars, 8)

            def norms(g):
                pool.wait_ge(diag_ready, g * 8 + 8)
                pool.tensor_tensor(exp_bias[:, :], norm2[:, :, GRAV], exponent_scale[:, :],
                                   ALU.mult).then_inc(cols_ready, 1)
                pool.tensor_copy(cols[:, :, GRAV], norm2[:, :, GRAV]).then_inc(cols_ready, 1)
                pool.tensor_scalar(clamped[:, :], norm2[:, :, LANG], EPS_DEG * EPS_DEG, None,
                                   ALU.max).then_inc(clamp_ready, 1)
                pool.wait_ge(clamp_ready, g + 1)
                pool.tensor_tensor(cols[:, :, LANG], clamped[:, :], minus_half[:, :],
                                   ALU.pow).then_inc(cols_ready, 1)
                pool.tensor_tensor(norm[:, :], clamped[:, :], plus_half[:, :], ALU.pow).then_inc(norm_ready, 1)
                pool.wait_ge(norm_ready, g * 2 + 1)
                pool.tensor_tensor(least_sum[:, :, LANG], norm[:, :], least_sum[:, :, GRAV],
                                   ALU.mult).then_inc(norm_ready, 1)

            def deviations(g):
                pool.wait_ge(moments_ready, g * TILES + TILES)
                pool.tensor_tensor(var_eps[:, :], moments[:, :, 1], ln_eps[:, :], ALU.add).then_inc(var_ready, 1)
                pool.wait_ge(var_ready, g + 1)
                pool.tensor_tensor(rstd[:, :], var_eps[:, :], minus_half[:, :], ALU.pow).then_inc(rstd_ready, 1)

            def turn(g, par):
                norms(g)
                deviations(g - 1)

            groups(pool, lambda g, par: norms(g), turn, turn)
            deviations(GROUPS - 1)

        @block.tensor
        def _(pe):
            def take(job):
                if not (isinstance(job, int) and job < RING):
                    pe.wait_ge(ring_drained, job - (RING - 1))

            def split3(psum, pairs):
                n = 0
                for a_hi, a_lo, b_hi, b_lo in pairs:
                    for a, b in ((a_hi, b_hi), (a_hi, b_lo), (a_lo, b_hi)):
                        n += 1
                        last = pe.matmul(psum, a, b, start=(n == 1), stop=(n == 3 * len(pairs)))
                return last

            def set_up_u(which):
                w = (w_hi[which], w_lo[which])
                for e in range(DC):
                    pe.wait_ge(w_lo_ready, which * DC + e + 1)
                    for i in range(DC):
                        for n, (a, b) in enumerate(((0, 0), (0, 1), (1, 0))):
                            last = pe.matmul(u_banks[which][i][:, i * P:], w[a][:, e, i * P:(i + 1) * P], w[b][:, e, i * P:],
                                             start=(e == 0 and n == 0), stop=(e == DC - 1 and n == 2))
                        if e == DC - 1:
                            last.then_inc(ring_filled, 1)

            def set_up_woT():
                pe.wait_ge(wo_loaded, 16)
                pe.wait_ge(ring_drained, DC)
                for f in range(DC):
                    for e in range(DC):
                        last = pe.transpose(ring[f][:, e * P:(e + 1) * P],
                                            w_rows[3][:, e, f * P:(f + 1) * P], ident[:, :])
                    last.then_inc(ring_filled, 1)

            def set_up_c():
                pe.wait_ge(w_lo_ready, 3 * DC)
                for i in range(DC):
                    take(C_JOB + i)
                    rows = slice(i * P, (i + 1) * P)
                    split3(ring[i][:, :], [(w_hi[2][:, f, rows], w_lo[2][:, f, rows], woT_hi[:, f, :], woT_lo[:, f, :])
                                           for f in range(DC)]).then_inc(ring_filled, 1)

            def x_transposes(job, off, g, par):
                pe.wait_ge(x_loaded[par], g * (8 * TILES) + 8 * TILES * (2 - par))
                for c in range(DC):
                    take(job + (off + c))
                    for t in range(TILES):
                        last = pe.transpose(ring[(off + c) % RING][:, t * P:(t + 1) * P],
                                            xs[par][:, t, c * P:(c + 1) * P], ident[:, :])
                    last.then_inc(ring_filled, 1)

            def z_job(job, k, par):
                which, j = divmod(k, DC)
                take(job + k)
                pairs = []
                for i in range(j + 1):
                    pairs.append((u_hi[:, which, i, j * P:(j + 1) * P], u_lo[:, which, i, j * P:(j + 1) * P],
                                  hT_hi[par][:, i, :], hT_lo[par][:, i, :]))
                split3(ring[k % RING][:, :], pairs).then_inc(ring_filled, 1)

            def v_job(job, off, t, par):
                take(job + off)
                tile = slice(t * P, (t + 1) * P)
                split3(ring[off % RING][:, :],
                       [(hT_hi[par][:, c, tile], hT_lo[par][:, c, tile], c_hi[:, c, :], c_lo[:, c, :])
                        for c in range(DC)]).then_inc(ring_filled, 1)

            def grams(job, g, par):
                for t in range(TILES):
                    tile = slice(t * P, (t + 1) * P)
                    for c in range(DC):
                        if t == 0:
                            pe.wait_ge(ring_drained, job + (DC + 1 + c))
                        for n, (a, b) in enumerate(((hT_hi, yT_hi), (hT_hi, yT_lo), (hT_lo, yT_hi))):
                            last = pe.matmul(gram[:, t, :, :], a[par][:, c, tile], b[:, c, :, tile],
                                             start=(c == 0 and n == 0), stop=(c == DC - 1 and n == 2))
                    if t % 2:
                        last.then_inc(gram_filled, 1)

            def raw_transposes(g):
                pe.wait_ge(raw_copied, g * 2 + 2)
                for t in range(TILES):
                    for w in range(2):
                        last = pe.transpose(small[:, t, w, :], raw[:, t, w, :], ident[:, :])
                last.then_inc(rawT_filled, 1)

            def spread(g):
                pe.wait_ge(cols_ready, g * 3 + 3)
                pe.wait_ge(sym_ready, g + 1)
                for t in range(TILES):
                    for w in range(2):
                        last = pe.transpose(small[:, t, w, :], cols[:, t, w:w + 1].to_broadcast([P, P]), ident[:, :])
                last.then_inc(spread_filled, 1)

            def k_transposes(g):
                pe.wait_ge(k_ready, g * TILES + TILES)
                for t in range(TILES):
                    last = pe.transpose(small[:, t // 2, t % 2, :], kmat[:, t, :], ident[:, :])
                last.then_inc(kT_filled, 1)

            def out_jobs(job, off, g):
                pe.wait_ge(kT_lo_ready, g + 1)
                for t in range(TILES):
                    take(job + (off + t))
                    split3(ring[(off + t) % RING][:, :],
                           [(kT_hi[:, t, :], kT_lo[:, t, :], v_hi[:, t, :], v_lo[:, t, :])]).then_inc(ring_filled, 1)

            def turn(g, par, post=True, ahead=True):
                job = first_job(g)
                for k in range(ZJOBS):
                    z_job(job, k, par)
                if post:
                    k_transposes(g - 1)
                grams(job, g, par)
                off = ZJOBS
                if post:
                    out_jobs(job, off, g - 1)
                    off += OJOBS
                v_job(job, off, 0, par)
                raw_transposes(g)
                v_job(job, off + 1, 1, par)
                if not ahead:
                    spread(g)
                v_job(job, off + 2, 2, par)
                v_job(job, off + 3, 3, par)
                if ahead:
                    x_transposes(job, off + VJOBS, g + 1, 1 - par)
                    spread(g)

            pe.wait_ge(consts, 7)
            set_up_u(LANG)
            set_up_u(GRAV)
            set_up_woT()
            x_transposes(XT0_JOB, 0, 0, 0)
            set_up_c()
            groups(pe, lambda g, par: turn(g, par, post=False), turn, lambda g, par: turn(g, par, ahead=False))
            k_transposes(GROUPS - 1)
            out_jobs(GROUPS * JOBS + (AHEAD - TJOBS), 0, GROUPS - 1)

        @block.scalar
        def _(act):
            def hi(job, dst, src, scale=1.0):
                act.wait_ge(ring_filled, job + 1)
                act.activation(dst, src, ACT.Copy, scale=scale).then_inc(hi_written, 1)

            def z_hi(job, k):
                which, j = divmod(k, DC)
                hi(job + k, yT_hi[:, j, which, :], ring[k % RING][:, :])

            def exps(g):
                act.wait_ge(dist_ready, g + 1)
                for t in range(TILES):
                    act.activation(expd[:, t, :], dist[:, t, :], ACT.Exp, bias=exp_bias[:, t:t + 1],
                                   scale=scal[:, 7:8]).then_inc(exp_ready, 1)

            def grav_scale(g):
                act.wait_ge(factor_ready, g * 2 + 2)
                for t in range(TILES):
                    act.activation(grav_s[:, t, :], att[:, t, GRAV, :], ACT.Copy,
                                   scale=factor[:, t, GRAV:GRAV + 1]).then_inc(grav_scaled, 1)

            def kT_hi_part(g):
                act.wait_ge(kT_filled, g + 1)
                act.activation(kT_hi[:, :, :], small[:, 0:2, :, :].rearrange("p t w m -> p (t w) m"),
                               ACT.Copy).then_inc(kT_hi_ready, 1)

            def v_his(job, off, tiles):
                for t in tiles:
                    hi(job + (off + t), v_hi[:, t, :], ring[(off + t) % RING][:, :])

            def turn(g, par, post=True, ahead=True):
                job = first_job(g)
                z_hi(job, 0)
                z_hi(job, 1)
                if post:
                    exps(g - 1)
                z_hi(job, 2)
                z_hi(job, 3)
                if post:
                    grav_scale(g - 1)
                for k in range(DC, ZJOBS):
                    z_hi(job, k)
                if post:
                    kT_hi_part(g - 1)
                for b in range(2):
                    act.wait_ge(gram_filled, g * 2 + (b + 1))
                    act.activation(raw[:, 2 * b:2 * b + 2, :, :], gram[:, 2 * b:2 * b + 2, :, :],
                                   ACT.Copy).then_inc(raw_copied, 1)
                off = ZJOBS + (OJOBS if post else 0)
                if ahead:
                    v_his(job, off, range(TILES))
                    for c in range(DC):
                        hi(job + (off + VJOBS + c), hT_hi[1 - par][:, c, :], ring[(off + c) % RING][:, :])
                else:
                    v_his(job, off, (0, 1))
                    exps(g)
                    v_his(job, off, (2, 3))

            for which in range(2):
                for e in range(DC):
                    act.wait_ge(w_loaded[which][e], 16)
                    act.activation(w_hi[which][:, e, :], w_rows[which][:, e, :], ACT.Copy).then_inc(w_hi_ready, 1)
            act.wait_ge(small_loaded, 64)
            act.activation(scal[:, 2:3], scal[:, 0:1], ACT.Exp, scale=-1.0).then_inc(sigma_exp, 1)
            act.activation(scal[:, 3:4], scal[:, 1:2], ACT.Exp).then_inc(sigma_exp, 1)
            for which in range(2):
                for i in range(DC):
                    bank = u_banks[which][i]
                    act.wait_ge(ring_filled, U_JOB + which * DC + i + 1)
                    a = act.activation(u_hi[:, which, i, i * P:(i + 1) * P], bank[:, i * P:(i + 1) * P],
                                       ACT.Copy, scale=0.5)
                    if i < DC - 1:
                        a = act.activation(u_hi[:, which, i, (i + 1) * P:], bank[:, (i + 1) * P:], ACT.Copy)
                    a.then_inc(hi_written, 1)
                if which == LANG:
                    act.wait_ge(wv_loaded, 16)
                    for e in range(DC):
                        act.activation(w_hi[2][:, e, :], w_rows[2][:, e, :], ACT.Copy).then_inc(w_hi_ready, 1)
            for f in range(DC):
                hi(WOT_JOB + f, woT_hi[:, f, :], ring[f][:, :])
            for c in range(DC):
                hi(XT0_JOB + c, hT_hi[0][:, c, :], ring[c][:, :])
            for i in range(DC):
                hi(C_JOB + i, c_hi[:, i, :], ring[i][:, :])
            groups(act, lambda g, par: turn(g, par, post=False), turn, lambda g, par: turn(g, par, ahead=False))
            grav_scale(GROUPS - 1)
            kT_hi_part(GROUPS - 1)

        @block.vector
        def _(dve):
            def lo(count, dst, src, hi_part):
                dve.wait_ge(hi_written, count)
                dve.tensor_tensor(dst, src, hi_part.bitcast(F32), ALU.subtract).then_inc(ring_drained, 1)

            def z_lo(base, k):
                which, j = divmod(k, DC)
                lo(base + (k + 1), yT_lo[:, j, which, :], ring[k % RING][:, :], yT_hi[:, j, which, :])

            def symmetric(g):
                dve.wait_ge(diag_ready, g * 8 + 8)
                dve.wait_ge(rawT_filled, g + 1)
                dve.tensor_tensor(sym[:, :, :, :], small[:, :, :, :], raw[:, :, :, :],
                                  ALU.add).then_inc(sym_ready, 1)
                dve.wait_ge(sym_ready, g + 1)
                dve.scalar_tensor_tensor(out=lang0[:, :, :], in0=sym[:, :, LANG, :], scalar=0.0,
                                         in1=over_tiles(mask), op0=ALU.max, op1=ALU.mult).then_inc(lang0_ready, 1)

            def diagonals(g):
                dve.wait_ge(raw_copied, g * 2 + 2)
                for t in range(TILES):
                    for w in range(2):
                        dve.tensor_tensor_reduce(sym[:, t, w, :], raw[:, t, w, :], ident[:, :], 2.0, 0.0, ALU.mult,
                                                 ALU.add, norm2[:, t, w:w + 1]).then_inc(diag_ready, 1)

            def distances(g):
                dve.wait_ge(spread_filled, g + 1)
                dve.scalar_tensor_tensor(out=dist[:, :, :], in0=sym[:, :, GRAV, :], scalar=-2.0,
                                         in1=small[:, :, GRAV, :], op0=ALU.mult, op1=ALU.add).then_inc(dist_ready, 1)
                dve.wait_ge(lang0_ready, g + 1)
                dve.tensor_tensor(att[:, :, LANG, :], lang0[:, :, :], small[:, :, LANG, :],
                                  ALU.mult).then_inc(lang_ready, 1)

            def gravity(g):
                dve.wait_ge(exp_ready, g * TILES + TILES)
                dve.scalar_tensor_tensor(out=att[:, :, GRAV, :], in0=expd[:, :, :], scalar=1.0,
                                         in1=over_tiles(mask), op0=ALU.min, op1=ALU.mult).then_inc(grav_ready, 1)
                dve.wait_ge(grav_ready, g + 1)
                dve.wait_ge(lang_ready, g + 1)
                dve.tensor_reduce(rowsum[:, :, :], att[:, :, :, :], AX_X, ALU.add).then_inc(sums_ready, 1)
                dve.wait_ge(norm_ready, g * 2 + 2)
                dve.wait_ge(sums_ready, g * 2 + 1)
                dve.tensor_tensor(deg[:, :, :], rowsum[:, :, :], least_sum[:, :, :], ALU.max).then_inc(sums_ready, 1)
                dve.wait_ge(sums_ready, g * 2 + 2)
                dve.reciprocal(deg_r[:, :, :], deg[:, :, :]).then_inc(factor_ready, 1)
                dve.wait_ge(factor_ready, g * 2 + 1)
                dve.tensor_tensor(factor[:, :, :], deg_r[:, :, :], w_pair[:, :, :],
                                  ALU.mult).then_inc(factor_ready, 1)

            def combine(g):
                dve.wait_ge(factor_ready, g * 2 + 2)
                dve.wait_ge(grav_scaled, g * TILES + TILES)
                for t in range(TILES):
                    dve.scalar_tensor_tensor(out=kmat[:, t, :], in0=att[:, t, LANG, :],
                                             scalar=factor[:, t, LANG:LANG + 1], in1=grav_s[:, t, :],
                                             op0=ALU.mult, op1=ALU.add).then_inc(k_ready, 1)

            def kT_lo_part(g):
                dve.wait_ge(kT_hi_ready, g + 1)
                dve.tensor_tensor(kT_lo[:, :, :], small[:, 0:2, :, :].rearrange("p t w m -> p (t w) m"),
                                  kT_hi[:, :, :].bitcast(F32), ALU.subtract).then_inc(kT_lo_ready, 1)

            def residual(job, off, g, par):
                if not isinstance(g, int) or g > 0:
                    dve.wait_ge(out_stored, g * (16 * TILES))
                for t in range(TILES):
                    dve.wait_ge(ring_filled, job + (off + t + 1))
                    dve.tensor_tensor(res[:, t, :], ring[(off + t) % RING][:, :], xs[par][:, t, :],
                                      ALU.add).then_inc(ring_drained, 1)
                for t in range(TILES):
                    dve.wait_ge(ring_drained, job + (off + t + 1))
                    dve.bn_stats(stats[:, t, :], res[:, t, :]).then_inc(stats_ready, 1)

            def aggregate():
                for t in range(TILES):
                    dve.bn_aggr(moments[:, t, :], stats[:, t, :]).then_inc(moments_ready, 1)

            def normalise(g):
                dve.wait_ge(rstd_ready, g + 1)
                for t in range(TILES):
                    dve.tensor_scalar(res[:, t, :], res[:, t, :], moments[:, t, 0:1], rstd[:, t:t + 1],
                                      ALU.subtract, ALU.mult).then_inc(out_ready, 1)

            def v_los(base, off, tiles):
                for t in tiles:
                    lo(base + (ZJOBS + t + 1), v_lo[:, t, :], ring[(off + t) % RING][:, :], v_hi[:, t, :])

            def turn(g, par, post=True, ahead=True):
                job = first_job(g)
                base = first_hi(g)
                z_lo(base, 0)
                if post:
                    distances(g - 1)
                z_lo(base, 1)
                z_lo(base, 2)
                if post:
                    gravity(g - 1)
                z_lo(base, 3)
                if post:
                    combine(g - 1)
                for k in range(DC, ZJOBS):
                    z_lo(base, k)
                off = ZJOBS
                if post:
                    kT_lo_part(g - 1)
                    residual(job, off, g - 1, 1 - par)
                    off += OJOBS
                    dve.wait_ge(stats_ready, g * TILES)
                diagonals(g)
                if post:
                    aggregate()
                v_los(base, off, (0,))
                symmetric(g)
                v_los(base, off, (1,))
                if not ahead:
                    distances(g)
                if post:
                    normalise(g - 1)
                v_los(base, off, (2,))
                if not ahead:
                    gravity(g)
                v_los(base, off, (3,))
                if ahead:
                    for c in range(DC):
                        lo(base + (ZJOBS + VJOBS + c + 1), hT_lo[1 - par][:, c, :], ring[(off + c) % RING][:, :],
                           hT_hi[1 - par][:, c, :])

            for which in range(2):
                for e in range(DC):
                    dve.wait_ge(w_hi_ready, which * DC + e + 1)
                    dve.tensor_tensor(w_lo[which][:, e, :], w_rows[which][:, e, :],
                                      w_hi[which][:, e, :].bitcast(F32), ALU.subtract).then_inc(w_lo_ready, 1)
            dve.wait_ge(sigma_exp, 2)
            dve.tensor_scalar(scal[:, 4:5], scal[:, 2:3], 1.0, None, ALU.add).then_inc(scalars, 1)
            dve.tensor_tensor(scal[:, 6:7], scal[:, 3:4], scal[:, 3:4], ALU.mult).then_inc(scalars, 1)
            dve.wait_ge(scalars, 2)
            dve.reciprocal(scal[:, 5:6], scal[:, 4:5]).then_inc(scalars, 1)
            dve.reciprocal(scal[:, 8:9], scal[:, 6:7]).then_inc(scalars, 1)
            dve.wait_ge(scalars, 4)
            dve.tensor_scalar(scal[:, 7:8], scal[:, 8:9], -0.5, None, ALU.mult).then_inc(scalars, 1)
            dve.tensor_copy(w_pair[:, :, 0], scal[:, 5:6].to_broadcast([P, TILES])).then_inc(scalars, 1)
            dve.wait_ge(scalars, 6)
            dve.tensor_scalar(w_pair[:, :, 1], w_pair[:, :, 0], -1.0, 1.0, ALU.mult, ALU.add).then_inc(scalars, 1)
            dve.wait_ge(scalars, 7)
            dve.tensor_copy(exponent_scale[:, :], scal[:, 7:8].to_broadcast([P, TILES])).then_inc(scalars, 1)

            dve.wait_ge(consts, 8)
            for which in range(2):
                for i in range(DC):
                    bank = u_banks[which][i]
                    dve.wait_ge(hi_written, U_JOB + which * DC + i + 1)
                    d = dve.scalar_tensor_tensor(
                        out=u_lo[:, which, i, i * P:(i + 1) * P], in0=bank[:, i * P:(i + 1) * P], scalar=0.5,
                        in1=u_hi[:, which, i, i * P:(i + 1) * P].bitcast(F32), op0=ALU.mult, op1=ALU.subtract)
                    if i < DC - 1:
                        d = dve.tensor_tensor(u_lo[:, which, i, (i + 1) * P:], bank[:, (i + 1) * P:],
                                              u_hi[:, which, i, (i + 1) * P:].bitcast(F32), ALU.subtract)
                    d.then_inc(ring_drained, 1)
                if which == LANG:
                    for e in range(DC):
                        dve.wait_ge(w_hi_ready, 2 * DC + e + 1)
                        dve.tensor_tensor(w_lo[2][:, e, :], w_rows[2][:, e, :], w_hi[2][:, e, :].bitcast(F32),
                                          ALU.subtract).then_inc(w_lo_ready, 1)
            for f in range(DC):
                lo(WOT_JOB + f + 1, woT_lo[:, f, :], ring[f][:, :], woT_hi[:, f, :])
            for c in range(DC):
                lo(XT0_JOB + c + 1, hT_lo[0][:, c, :], ring[c][:, :], hT_hi[0][:, c, :])
            for i in range(DC):
                lo(C_JOB + i + 1, c_lo[:, i, :], ring[i][:, :], c_hi[:, i, :])
            groups(dve, lambda g, par: turn(g, par, post=False), turn, lambda g, par: turn(g, par, ahead=False))
            combine(GROUPS - 1)
            kT_lo_part(GROUPS - 1)
            residual(GROUPS * JOBS + (AHEAD - TJOBS), 0, GROUPS - 1, 1)
            dve.wait_ge(stats_ready, GROUPS * TILES)
            aggregate()
            normalise(GROUPS - 1)


_INS = ['x', 'adj', 'L0_gnn_W_lang', 'L0_gnn_W_grav', 'L0_gnn_W_V', 'L0_gnn_W_O',
        'L0_gnn_gate_logit', 'L0_gnn_log_sigma']


def kernel(**inputs):
    import numpy as _np
    import concourse.bacc as _bacc
    from concourse import mybir as _mybir
    from concourse.bass_utils import run_bass_kernel_spmd as _run

    nc = _bacc.Bacc("TRN2", target_bir_lowering=False, num_devices=1)
    arrays, args = {}, []
    for name in _INS:
        a = _np.ascontiguousarray(inputs[name])
        if a.ndim == 0:
            a = a.reshape(1)
        arrays[f"in_{name}_dram"] = a
        args.append(nc.dram_tensor(f"in_{name}_dram", a.shape, _mybir.dt.from_np(a.dtype), kind="ExternalInput").ap())
    shape = inputs["x"].shape
    args.append(nc.dram_tensor("out_0_dram", shape, _mybir.dt.float32, kind="ExternalOutput").ap())
    adj_resnorm(nc, *args)
    r = _run(nc, [arrays], core_ids=[0])
    return r.results[0]["out_0_dram"]
```

```python
from contextlib import ExitStack

import concourse.bass as bass
from concourse import mybir
from concourse.alu_op_type import AluOpType as ALU

ACT = mybir.ActivationFunctionType
F32 = mybir.dt.float32
F32R = mybir.dt.float32r
AX_X = mybir.AxisListType.X

P = 128
EPS_DEG = 1e-8
EPS_LN = 1e-5
LANG, GRAV = 0, 1


def adj_resnorm(nc, x, adj, w_lang, w_grav, w_v, w_o, gate_logit, log_sigma, out):
    NGRAPH, N, D = x.shape
    DC = D // P
    TILES = 4
    ROWS = TILES * P
    GROUPS = NGRAPH * N // ROWS
    RING = 4
    ZJOBS, VJOBS, TJOBS, OJOBS = 2 * DC, TILES, DC, TILES
    JOBS = ZJOBS + VJOBS + TJOBS + OJOBS
    HI_JOBS = ZJOBS + VJOBS + TJOBS
    U_JOB, WOT_JOB, XT0_JOB, C_JOB = (0, 2 * DC + TJOBS), DC, 2 * DC, 3 * DC + TJOBS
    SETUP_JOBS = 2 * DC + DC + DC
    assert ROWS == 512 and P == 2 * N and D == 512 and JOBS % RING == 0 and SETUP_JOBS % RING == 0
    assert GROUPS % 2 == 0 and GROUPS >= 4

    x_rows = x.rearrange("(g t a) n d -> g t (a n) d", t=TILES, a=2)
    out_rows = out.rearrange("(g t a) n d -> g t (a n) d", t=TILES, a=2)

    AHEAD = SETUP_JOBS

    def first_job(g):
        return AHEAD + OJOBS if isinstance(g, int) and g == 0 else g * JOBS + AHEAD

    def first_hi(g):
        return g * HI_JOBS + (SETUP_JOBS + TJOBS)

    with ExitStack() as ctx:
        def sb(name, shape, dt=F32):
            return ctx.enter_context(nc.sbuf_tensor(name, shape, dt))

        def sem(name):
            return ctx.enter_context(nc.semaphore(name))

        ring = [ctx.enter_context(nc.psum_tensor(f"ring{i}", [P, 512], F32)) for i in range(RING)]
        gram = ctx.enter_context(nc.psum_tensor("gram", [P, TILES, 2, P], F32))
        trans = ctx.enter_context(nc.psum_tensor("trans", [P, TILES, P], F32))
        spread_ps = ctx.enter_context(nc.psum_tensor("spread_ps", [P, TILES, 2, N], F32))

        u_banks = [[bank[:, :] for bank in ring],
                   [gram[:, i:i + 2, :, :].rearrange("p t w m -> p (t w m)") for i in (0, 2)]
                   + [trans[:, :, :].rearrange("p t m -> p (t m)"),
                      spread_ps[:, :, :, :].rearrange("p t w m -> p (t w m)")]]

        ident = sb("ident", [P, P])
        ident_own = sb("ident_own", [P, N])
        adj_own = sb("adj_own", [P, N])
        not_eye = sb("not_eye", [P, N])
        mask = sb("mask", [P, N])
        same_graph = sb("same_graph", [P, P], F32R)
        scal = sb("scal", [P, 9])
        exponent_scale = sb("exponent_scale", [P, TILES])
        w_pair = sb("w_pair", [P, TILES, 2])
        minus_half = sb("minus_half", [P, TILES])
        plus_half = sb("plus_half", [P, TILES])
        ln_eps = sb("ln_eps", [P, TILES])
        w_rows = [sb(f"w_rows{i}", [P, DC, D]) for i in range(4)]
        u_hi = sb("u_hi", [P, 2, DC, D], F32R)
        u_lo = sb("u_lo", [P, 2, DC, D], F32R)
        c_hi = sb("c_hi", [P, DC, D], F32R)
        c_lo = sb("c_lo", [P, DC, D], F32R)

        xs = [sb(f"x{i}", [P, TILES, D]) for i in range(2)]
        hT_hi = [sb(f"hT_hi{i}", [P, DC, ROWS], F32R) for i in range(2)]
        hT_lo = [sb(f"hT_lo{i}", [P, DC, ROWS], F32R) for i in range(2)]
        yT_hi = sb("yT_hi", [P, DC, 2, ROWS], F32R)
        yT_lo = sb("yT_lo", [P, DC, 2, ROWS], F32R)
        v_hi = sb("v_hi", [P, TILES, D], F32R)
        v_lo = sb("v_lo", [P, TILES, D], F32R)
        w_hi = [yT_hi[:, :, i, :] for i in range(2)] + [v_hi[:, :, :]]
        w_lo = [yT_lo[:, :, i, :] for i in range(2)] + [v_lo[:, :, :]]
        woT_hi, woT_lo = hT_hi[1], hT_lo[1]
        def over_w(which, chunk):
            return w_rows[which][:, chunk, :].rearrange("p (t w m) -> p t w m", w=2, m=N)

        def half(which, chunk, i):
            return w_rows[which][:, chunk, i * TILES * N:(i + 1) * TILES * N].rearrange("p (t m) -> p t m", m=N)

        raw = over_w(0, 0)
        sym = over_w(0, 1)
        att = over_w(0, 2)
        att_s = over_w(0, 3)
        diag = over_w(1, 0)
        lang0 = half(1, 1, 0)
        dist = half(1, 1, 1)
        expd = half(1, 2, 0)
        norm2 = sb("norm2", [P, TILES, 2])
        cols = sb("cols", [P, TILES, 2])
        cols_r = sb("cols_r", [P, 2, TILES, 2], F32R)
        cols_d = sb("cols_d", [P, 2, TILES, 2, N], F32R)
        clamped = sb("clamped", [P, TILES])
        exp_bias = sb("exp_bias", [P, TILES])
        rowsum = sb("rowsum", [P, TILES, 2])
        norm = sb("norm", [P, TILES])
        least_sum = sb("least_sum", [P, TILES, 2])
        deg = sb("deg", [P, TILES, 2])
        deg_r = sb("deg_r", [P, TILES, 2])
        factor = sb("factor", [P, TILES, 2])
        kmat = sb("kmat", [P, TILES, P])
        kT_hi = sb("kT_hi", [P, TILES, P], F32R)
        kT_lo = sb("kT_lo", [P, TILES, P], F32R)
        res = w_rows[2:4]
        stats = sb("stats", [P, TILES, 6])
        moments = sb("moments", [P, TILES, 2])
        var_eps = sb("var_eps", [P, TILES])
        minus_mean = sb("minus_mean", [P, TILES])
        rstd = sb("rstd", [P, TILES])
        rstd_last = sb("rstd_last", [P, TILES])
        shift = sb("shift", [P, TILES])

        w_loaded = [[sem(f"w_loaded{i}_{e}") for e in range(DC)] for i in range(2)]
        wv_loaded = sem("wv_loaded")
        wo_loaded = sem("wo_loaded")
        w_hi_ready = sem("w_hi_ready")
        w_lo_ready = sem("w_lo_ready")
        small_loaded = sem("small_loaded")
        x_loaded = [sem(f"x_loaded{i}") for i in range(2)]
        out_stored = sem("out_stored")
        warm_up_ready = sem("warm_up_ready")
        consts = sem("consts")
        own_ready = sem("own_ready")
        scalars = sem("scalars")
        sigma_exp = sem("sigma_exp")
        ring_filled = sem("ring_filled")
        hi_written = sem("hi_written")
        ring_drained = sem("ring_drained")
        gram_filled = sem("gram_filled")
        raw_copied = sem("raw_copied")
        rawT_filled = sem("rawT_filled")
        sym_ready = sem("sym_ready")
        diag_ready = sem("diag_ready")
        cols_r_ready = sem("cols_r_ready")
        cols_d_ready = sem("cols_d_ready")
        clamp_ready = sem("clamp_ready")
        cols_ready = sem("cols_ready")
        norm_ready = sem("norm_ready")
        spread_filled = sem("spread_filled")
        lang0_ready = sem("lang0_ready")
        lang_ready = sem("lang_ready")
        dist_ready = sem("dist_ready")
        exp_ready = sem("exp_ready")
        grav_ready = sem("grav_ready")
        sums_ready = sem("sums_ready")
        factor_ready = sem("factor_ready")
        scaled_ready = sem("scaled_ready")
        k_ready = sem("k_ready")
        kT_filled = sem("kT_filled")
        kT_hi_ready = sem("kT_hi_ready")
        kT_lo_ready = sem("kT_lo_ready")
        stats_ready = sem("stats_ready")
        moments_ready = sem("moments_ready")
        var_ready = sem("var_ready")
        rstd_ready = sem("rstd_ready")
        shift_ready = sem("shift_ready")
        out_ready = sem("out_ready")
        last_ready = sem("last_ready")

        def over_tiles(a):
            return a[:, :].rearrange("p (t m) -> p t m", t=1).to_broadcast([P, TILES, N])

        def own(a, graph, *index):
            return a[(slice(graph * N, (graph + 1) * N), *index, slice(graph * N, (graph + 1) * N))]

        def groups(eng, first, middle, last):
            first(0, 0)
            with eng.Fori(0, GROUPS // 2 - 1) as pair:
                middle(pair * 2 + 1, 1)
                middle(pair * 2 + 2, 0)
            last(GROUPS - 1, 1)

        block = ctx.enter_context(nc.Block())

        @block.sync
        def _(sp):
            for which, w in enumerate((w_lang, w_grav)):
                for e in range(DC):
                    sp.dma_start(w_rows[which][:, e, :], w[e * P:(e + 1) * P, :]).then_inc(w_loaded[which][e], 16)
            for t in range(TILES):
                sp.dma_start(xs[0][:, t, :], x_rows[0, t]).then_inc(x_loaded[0], 16)
            sp.dma_start(w_rows[3][:, :, :], w_o.rearrange("(c p) d -> p c d", p=P)).then_inc(wo_loaded, 16)
            sp.dma_start(w_rows[2][:, :, :], w_v.rearrange("(c p) d -> p c d", p=P)).then_inc(wv_loaded, 16)
            for t in range(TILES):
                sp.dma_start(xs[1][:, t, :], x_rows[1, t]).then_inc(x_loaded[1], 16)

            def load(g, par):
                for t in range(TILES):
                    sp.wait_ge(ring_drained, first_job(g) + (ZJOBS + t + 1))
                    src = x_rows[bass.ds(g + 1, 1), t].rearrange("g p d -> (g p) d")
                    sp.dma_start(xs[1 - par][:, t, :], src).then_inc(x_loaded[1 - par], 16)

            def store(g, par, last=False):
                for t in range(TILES):
                    if last:
                        sp.wait_ge(last_ready, t + 1)
                    else:
                        sp.wait_ge(out_ready, g * TILES + (t + 1))
                    dst = out_rows[bass.ds(g, 1), t].rearrange("g p d -> (g p) d")
                    sp.dma_start(dst, res[par][:, t, :]).then_inc(out_stored, 16)

            def turn(g, par):
                load(g, par)
                store(g - 1, 1 - par)

            groups(sp, lambda g, par: None, turn, lambda g, par: store(g - 1, 1 - par))
            store(GROUPS - 1, 1, last=True)
            sp.wait_ge(out_stored, 16 * TILES * GROUPS)

        @block.gpsimd
        def _(pool):
            pool.memset(ident[:, :], 0.0).then_inc(consts, 1)
            pool.memset(same_graph[:, :].bitcast(F32), 0.0).then_inc(consts, 1)
            pool.memset(kmat[:, :, :], 0.0).then_inc(consts, 1)
            pool.memset(minus_half[:, :], -0.5).then_inc(consts, 1)
            pool.memset(plus_half[:, :], 0.5).then_inc(consts, 1)
            pool.memset(ln_eps[:, :], EPS_LN).then_inc(consts, 1)
            pool.memset(least_sum[:, :, :], EPS_DEG).then_inc(consts, 1)
            pool.wait_ge(consts, 7)
            pool.affine_select(out=ident[:, :], in_=ident[:, :], compare_op=ALU.not_equal, fill=1.0,
                               base=0, pattern=[[-1, P]], channel_multiplier=1).then_inc(consts, 1)
            for a in range(2):
                pool.dma_start(adj_own[a * N:(a + 1) * N, :], adj).then_inc(small_loaded, 16)
            pool.dma_start(scal[:, 0:1], gate_logit.partition_broadcast(P)).then_inc(small_loaded, 16)
            pool.dma_start(scal[:, 1:2], log_sigma.partition_broadcast(P)).then_inc(small_loaded, 16)
            pool.wait_ge(own_ready, 4)
            pool.tensor_scalar(not_eye[:, :], ident_own[:, :], -1.0, 1.0, ALU.mult, ALU.add).then_inc(consts, 1)
            pool.wait_ge(consts, 9)
            pool.wait_ge(small_loaded, 64)
            pool.tensor_tensor(mask[:, :], adj_own[:, :], not_eye[:, :], ALU.mult).then_inc(consts, 1)
            pool.wait_ge(scalars, 8)

            def norms(g):
                pool.wait_ge(diag_ready, g * 2 + 2)
                pool.tensor_tensor(exp_bias[:, :], norm2[:, :, GRAV], exponent_scale[:, :],
                                   ALU.mult).then_inc(cols_ready, 1)
                pool.tensor_scalar(clamped[:, :], norm2[:, :, LANG], EPS_DEG * EPS_DEG, None,
                                   ALU.max).then_inc(clamp_ready, 1)
                pool.tensor_copy(cols[:, :, GRAV], norm2[:, :, GRAV]).then_inc(cols_ready, 1)
                pool.wait_ge(clamp_ready, g + 1)
                pool.tensor_tensor(cols[:, :, LANG], clamped[:, :], minus_half[:, :],
                                   ALU.pow).then_inc(cols_ready, 1)
                pool.tensor_tensor(norm[:, :], clamped[:, :], plus_half[:, :], ALU.pow).then_inc(norm_ready, 1)
                pool.wait_ge(norm_ready, g * 2 + 1)
                pool.tensor_tensor(least_sum[:, :, LANG], norm[:, :], least_sum[:, :, GRAV],
                                   ALU.mult).then_inc(norm_ready, 1)

            def deviations(g):
                pool.wait_ge(moments_ready, g * TILES + TILES)
                pool.tensor_tensor(var_eps[:, :], moments[:, :, 1], ln_eps[:, :], ALU.add).then_inc(var_ready, 1)
                pool.tensor_scalar(minus_mean[:, :], moments[:, :, 0], -1.0, None, ALU.mult).then_inc(var_ready, 1)
                pool.wait_ge(var_ready, g * 2 + 2)
                pool.tensor_tensor(rstd[:, :], var_eps[:, :], minus_half[:, :], ALU.pow).then_inc(rstd_ready, 1)
                pool.wait_ge(rstd_ready, g + 1)
                pool.tensor_tensor(shift[:, :], minus_mean[:, :], rstd[:, :], ALU.mult).then_inc(shift_ready, 1)

            def turn(g, par):
                deviations(g - 1)
                norms(g)

            def last_turn(g, par):
                norms(g)
                deviations(g - 1)

            groups(pool, lambda g, par: norms(g), turn, last_turn)
            for t in range(TILES):
                pool.wait_ge(moments_ready, (GROUPS - 1) * TILES + t + 1)
                pool.tensor_tensor(var_eps[:, t:t + 1], moments[:, t, 1:2], ln_eps[:, t:t + 1],
                                   ALU.add).then_inc(var_ready, 1)
                pool.wait_ge(var_ready, (GROUPS - 1) * 2 + t + 1)
                pool.tensor_tensor(rstd_last[:, t:t + 1], var_eps[:, t:t + 1], minus_half[:, t:t + 1],
                                   ALU.pow).then_inc(rstd_ready, 1)

        @block.tensor
        def _(pe):
            def take(job):
                if not (isinstance(job, int) and job < RING):
                    pe.wait_ge(ring_drained, job - (RING - 1))

            def split3(psum, pairs, first=True, final=True):
                n = 0
                for a_hi, a_lo, b_hi, b_lo in pairs:
                    for a, b in ((a_hi, b_hi), (a_hi, b_lo), (a_lo, b_hi)):
                        n += 1
                        last = pe.matmul(psum, a, b, start=(first and n == 1), stop=(final and n == 3 * len(pairs)))
                return last

            def warm_up(n):
                pe.wait_ge(warm_up_ready, 1)
                for _ in range(n):
                    pe.matmul(gram[:, 0, :, :], hT_hi[1][:, 0, 0:P], hT_hi[1][:, 0, 0:2 * P], start=True, stop=True)

            def set_up_u(which, chunks):
                w = (w_hi[which], w_lo[which])
                for e in chunks:
                    pe.wait_ge(w_hi_ready, which * DC + e + 1)
                    for n, (a, b) in enumerate(((0, 0), (0, 1), (1, 0))):
                        if n == 1:
                            pe.wait_ge(w_lo_ready, which * DC + e + 1)
                        for i in range(DC):
                            mm = pe.matmul(u_banks[which][i][:, i * P:], w[a][:, e, i * P:(i + 1) * P],
                                           w[b][:, e, i * P:], start=(e == 0 and n == 0), stop=(e == DC - 1 and n == 2))
                            if e == DC - 1 and n == 2:
                                mm.then_inc(ring_filled, 1)

            def set_up_woT():
                pe.wait_ge(wo_loaded, 16)
                for f in range(DC):
                    take(WOT_JOB + f)
                    for e in range(DC):
                        last = pe.transpose(ring[f][:, e * P:(e + 1) * P],
                                            w_rows[3][:, e, f * P:(f + 1) * P], ident[:, :])
                    last.then_inc(ring_filled, 1)

            def set_up_c():
                pe.wait_ge(w_lo_ready, 3 * DC)
                for i in range(DC):
                    pe.wait_ge(ring_drained, XT0_JOB + i + 1)
                    rows = slice(i * P, (i + 1) * P)
                    split3(ring[i][:, :], [(w_hi[2][:, f, rows], w_lo[2][:, f, rows], woT_hi[:, f, :], woT_lo[:, f, :])
                                           for f in range(DC)]).then_inc(ring_filled, 1)

            def x_transposes(job, off, g, par, chunks):
                pe.wait_ge(x_loaded[par], g * (8 * TILES) + 8 * TILES * (2 - par))
                for c in chunks:
                    take(job + (off + c))
                    for t in range(TILES):
                        last = pe.transpose(ring[(off + c) % RING][:, t * P:(t + 1) * P],
                                            xs[par][:, t, c * P:(c + 1) * P], ident[:, :])
                    last.then_inc(ring_filled, 1)

            def z_job(job, k, par):
                which, j = divmod(k, DC)
                take(job + k)
                pairs = []
                for i in range(j + 1):
                    pairs.append((u_hi[:, which, i, j * P:(j + 1) * P], u_lo[:, which, i, j * P:(j + 1) * P],
                                  hT_hi[par][:, i, :], hT_lo[par][:, i, :]))
                split3(ring[k % RING][:, :], pairs).then_inc(ring_filled, 1)

            def v_part(off, t, par, chunks):
                tile = slice(t * P, (t + 1) * P)
                return split3(ring[off % RING][:, :],
                              [(hT_hi[par][:, c, tile], hT_lo[par][:, c, tile], c_hi[:, c, :], c_lo[:, c, :])
                               for c in chunks], first=(chunks[0] == 0), final=(chunks[-1] == DC - 1))

            def v_job(job, off, t, par):
                take(job + off)
                v_part(off, t, par, range(DC)).then_inc(ring_filled, 1)

            def gram_part(t, par, chunks):
                tile = slice(t * P, (t + 1) * P)
                for c in chunks:
                    for n, (a, b) in enumerate(((hT_hi, yT_hi), (hT_hi, yT_lo), (hT_lo, yT_hi))):
                        last = pe.matmul(gram[:, t, :, :], a[par][:, c, tile], b[:, c, :, tile],
                                         start=(c == 0 and n == 0), stop=(c == DC - 1 and n == 2))
                return last

            def grams(job, g, par, post):
                early = range(DC - 1)
                for c in early:
                    pe.wait_ge(ring_drained, job + (DC + 1 + c))
                    gram_part(0, par, (c,))
                gram_part(2, par, early)
                if post:
                    k_transposes(g - 1)
                pe.wait_ge(ring_drained, job + ZJOBS)
                gram_part(0, par, (DC - 1,))
                gram_part(1, par, range(DC)).then_inc(gram_filled, 1)
                gram_part(2, par, (DC - 1,))
                gram_part(3, par, range(DC)).then_inc(gram_filled, 1)

            def raw_transposes(g):
                pe.wait_ge(raw_copied, g * 4 + 4)
                for t in range(TILES):
                    last = pe.transpose(trans[:, t, :], raw[:, t, :, :].rearrange("p w m -> p (w m)"), ident[:, :])
                last.then_inc(rawT_filled, 1)

            def spread(g):
                pe.wait_ge(cols_d_ready, g * 2 + 2)
                for part in range(2):
                    last = pe.matmul(spread_ps[:, :, :, :].rearrange("p t w m -> p (t w m)"), same_graph[:, :],
                                     cols_d[:, part].rearrange("p t w m -> p (t w m)"),
                                     start=(part == 0), stop=(part == 1))
                last.then_inc(spread_filled, 1)

            def k_transposes(g):
                pe.wait_ge(k_ready, g * 2 + 2)
                for t in range(TILES):
                    last = pe.transpose(trans[:, t, :], kmat[:, t, :], ident[:, :])
                last.then_inc(kT_filled, 1)

            def out_jobs(job, off, g):
                pe.wait_ge(kT_lo_ready, g + 1)
                for t in range(TILES):
                    take(job + (off + t))
                    split3(ring[(off + t) % RING][:, :],
                           [(kT_hi[:, t, :], kT_lo[:, t, :], v_hi[:, t, :], v_lo[:, t, :])]).then_inc(ring_filled, 1)

            def turn(g, par, post=True, ahead=True):
                job = first_job(g)
                for k in range(ZJOBS):
                    z_job(job, k, par)
                grams(job, g, par, post)
                off = ZJOBS
                if post:
                    out_jobs(job, off, g - 1)
                    off += OJOBS
                if ahead:
                    v_job(job, off, 0, par)
                    raw_transposes(g)
                    for t in range(1, TILES):
                        v_job(job, off + t, t, par)
                    x_transposes(job, off + VJOBS, g + 1, 1 - par, range(DC - 1))
                    spread(g)
                    x_transposes(job, off + VJOBS, g + 1, 1 - par, (DC - 1,))
                else:
                    raw_transposes(g)
                    v_job(job, off, 0, par)
                    spread(g)
                    v_job(job, off + 1, 1, par)
                    v_job(job, off + 2, 2, par)
                    take(job + (off + 3))
                    v_part(off + 3, 3, par, range(DC // 2))
                    k_transposes(g)
                    v_part(off + 3, 3, par, range(DC // 2, DC)).then_inc(ring_filled, 1)

            warm_up(12)
            set_up_u(LANG, range(DC))
            set_up_u(GRAV, range(DC // 2))
            pe.wait_ge(consts, 8)
            set_up_woT()
            set_up_u(GRAV, range(DC // 2, DC - 1))
            x_transposes(XT0_JOB, 0, 0, 0, range(DC))
            set_up_u(GRAV, (DC - 1,))
            set_up_c()
            pe.wait_ge(own_ready, 4)
            groups(pe, lambda g, par: turn(g, par, post=False), turn, lambda g, par: turn(g, par, ahead=False))
            out_jobs(GROUPS * JOBS + (AHEAD - TJOBS), 0, GROUPS - 1)

        @block.scalar
        def _(act):
            def hi(job, dst, src, scale=1.0):
                act.wait_ge(ring_filled, job + 1)
                act.activation(dst, src, ACT.Copy, scale=scale).then_inc(hi_written, 1)

            def z_hi(job, k):
                which, j = divmod(k, DC)
                hi(job + k, yT_hi[:, j, which, :], ring[k % RING][:, :])

            def exps(g):
                act.wait_ge(dist_ready, g + 1)
                for t in range(TILES):
                    act.activation(expd[:, t, :], dist[:, t, :], ACT.Exp, bias=exp_bias[:, t:t + 1],
                                   scale=scal[:, 7:8]).then_inc(exp_ready, 1)

            def kT_hi_part(g):
                act.wait_ge(kT_filled, g + 1)
                act.activation(kT_hi[:, :, :], trans[:, :, :], ACT.Copy).then_inc(kT_hi_ready, 1)

            def normalise_tile(count, t, par):
                act.wait_ge(shift_ready, count)
                act.activation(res[par][:, t, :], res[par][:, t, :], ACT.Identity, bias=shift[:, t:t + 1],
                               scale=rstd[:, t:t + 1]).then_inc(out_ready, 1)

            def v_his(job, off, tiles):
                for t in tiles:
                    hi(job + (off + t), v_hi[:, t, :], ring[(off + t) % RING][:, :])

            def turn(g, par, post=True, ahead=True):
                job = first_job(g)
                z_hi(job, 0)
                z_hi(job, 1)
                if post:
                    exps(g - 1)
                for k in range(2, ZJOBS):
                    z_hi(job, k)
                if post:
                    kT_hi_part(g - 1)
                for b in range(2):
                    act.wait_ge(gram_filled, g * 2 + (b + 1))
                    tiles = slice(2 * b, 2 * b + 2)
                    for a in range(2):
                        act.activation(raw[a * N:(a + 1) * N, tiles, :, :], own(gram, a, tiles, slice(0, 2)),
                                       ACT.Copy).then_inc(raw_copied, 1)
                off = ZJOBS + (OJOBS if post else 0)
                if ahead:
                    if post:
                        v_his(job, off, (0, 1))
                        for t in (0, 1):
                            normalise_tile(g, t, 1 - par)
                        v_his(job, off, (2,))
                        for t in (2, 3):
                            normalise_tile(g, t, 1 - par)
                        v_his(job, off, (3,))
                    else:
                        v_his(job, off, range(TILES))
                    for c in range(DC):
                        hi(job + (off + VJOBS + c), hT_hi[1 - par][:, c, :], ring[(off + c) % RING][:, :])
                else:
                    v_his(job, off, (0,))
                    exps(g)
                    v_his(job, off, (1, 2))
                    kT_hi_part(g)
                    v_his(job, off, (3,))
                    for t in range(TILES):
                        normalise_tile(g, t, 1 - par)

            for which in range(2):
                for e in range(DC):
                    act.wait_ge(w_loaded[which][e], 16)
                    act.activation(w_hi[which][:, e, :], w_rows[which][:, e, :], ACT.Copy).then_inc(w_hi_ready, 1)
            act.wait_ge(small_loaded, 64)
            act.activation(scal[:, 2:3], scal[:, 0:1], ACT.Exp, scale=-1.0).then_inc(sigma_exp, 1)
            act.activation(scal[:, 3:4], scal[:, 1:2], ACT.Exp).then_inc(sigma_exp, 1)

            def u_his(which):
                for i in range(DC):
                    bank = u_banks[which][i]
                    act.wait_ge(ring_filled, U_JOB[which] + i + 1)
                    a = act.activation(u_hi[:, which, i, i * P:(i + 1) * P], bank[:, i * P:(i + 1) * P],
                                       ACT.Copy, scale=0.5)
                    if i < DC - 1:
                        a = act.activation(u_hi[:, which, i, (i + 1) * P:], bank[:, (i + 1) * P:], ACT.Copy)
                    a.then_inc(hi_written, 1)

            u_his(LANG)
            for f in range(DC):
                hi(WOT_JOB + f, woT_hi[:, f, :], ring[f][:, :])
            act.wait_ge(wv_loaded, 16)
            for e in range(DC):
                act.activation(w_hi[2][:, e, :], w_rows[2][:, e, :], ACT.Copy).then_inc(w_hi_ready, 1)
            for c in range(DC):
                hi(XT0_JOB + c, hT_hi[0][:, c, :], ring[c][:, :])
            u_his(GRAV)
            for i in range(DC):
                hi(C_JOB + i, c_hi[:, i, :], ring[i][:, :])
            groups(act, lambda g, par: turn(g, par, post=False), turn, lambda g, par: turn(g, par, ahead=False))

        @block.vector
        def _(dve):
            def lo(count, dst, src, hi_part):
                dve.wait_ge(hi_written, count)
                dve.tensor_tensor(dst, src, hi_part.bitcast(F32), ALU.subtract).then_inc(ring_drained, 1)

            def z_lo(base, k):
                which, j = divmod(k, DC)
                lo(base + (k + 1), yT_lo[:, j, which, :], ring[k % RING][:, :], yT_hi[:, j, which, :])

            def symmetric(g):
                dve.wait_ge(diag_ready, g * 2 + 2)
                dve.wait_ge(rawT_filled, g + 1)
                for a in range(2):
                    rows = slice(a * N, (a + 1) * N)
                    for w in range(2):
                        dve.tensor_tensor(sym[rows, :, w, :], trans[w * N:(w + 1) * N, :, rows],
                                          raw[rows, :, w, :], ALU.add).then_inc(sym_ready, 1)
                dve.wait_ge(sym_ready, g * 4 + 4)
                dve.scalar_tensor_tensor(out=lang0[:, :, :], in0=sym[:, :, LANG, :], scalar=0.0,
                                         in1=over_tiles(mask), op0=ALU.max, op1=ALU.mult).then_inc(lang0_ready, 1)

            def diagonals(g):
                dve.wait_ge(raw_copied, g * 4 + 4)
                dve.scalar_tensor_tensor(out=diag[:, :, :, :].rearrange("p t w m -> p (t w) m"),
                                         in0=raw[:, :, :, :].rearrange("p t w m -> p (t w) m"), scalar=2.0,
                                         in1=ident_own[:, :].rearrange("p (t m) -> p t m", t=1)
                                         .to_broadcast([P, 2 * TILES, N]),
                                         op0=ALU.mult, op1=ALU.mult).then_inc(diag_ready, 1)

            def squared_norms(g):
                dve.wait_ge(diag_ready, g * 2 + 1)
                dve.tensor_reduce(norm2[:, :, :], diag[:, :, :, :], AX_X, ALU.add).then_inc(diag_ready, 1)

            def columns(g):
                dve.wait_ge(cols_ready, g * 3 + 3)
                dve.tensor_copy(cols_r[:, 0], cols[:, :, :]).then_inc(cols_r_ready, 1)
                dve.wait_ge(cols_r_ready, g * 2 + 1)
                dve.tensor_tensor(cols_r[:, 1], cols[:, :, :], cols_r[:, 0].bitcast(F32),
                                  ALU.subtract).then_inc(cols_r_ready, 1)
                dve.wait_ge(cols_r_ready, g * 2 + 2)
                for part in range(2):
                    dve.tensor_tensor(cols_d[:, part].rearrange("p t w m -> p (t w) m"),
                                      ident_own[:, :].rearrange("p (t m) -> p t m", t=1)
                                      .to_broadcast([P, 2 * TILES, N]),
                                      cols_r[:, part].bitcast(F32).rearrange("p t (w m) -> p (t w) m", m=1)
                                      .to_broadcast([P, 2 * TILES, N]), ALU.mult).then_inc(cols_d_ready, 1)

            def distances(g):
                dve.wait_ge(spread_filled, g + 1)
                dve.scalar_tensor_tensor(out=dist[:, :, :], in0=sym[:, :, GRAV, :], scalar=-2.0,
                                         in1=spread_ps[:, :, GRAV, :], op0=ALU.mult,
                                         op1=ALU.add).then_inc(dist_ready, 1)
                dve.wait_ge(lang0_ready, g + 1)
                dve.tensor_tensor(att[:, :, LANG, :], lang0[:, :, :], spread_ps[:, :, LANG, :],
                                  ALU.mult).then_inc(lang_ready, 1)

            def gravity(g):
                dve.wait_ge(exp_ready, g * TILES + TILES)
                dve.scalar_tensor_tensor(out=att[:, :, GRAV, :], in0=expd[:, :, :], scalar=1.0,
                                         in1=over_tiles(mask), op0=ALU.min, op1=ALU.mult).then_inc(grav_ready, 1)
                dve.wait_ge(grav_ready, g + 1)
                dve.wait_ge(lang_ready, g + 1)
                dve.tensor_reduce(rowsum[:, :, :], att[:, :, :, :], AX_X, ALU.add).then_inc(sums_ready, 1)
                dve.wait_ge(norm_ready, g * 2 + 2)
                dve.wait_ge(sums_ready, g * 2 + 1)
                dve.tensor_tensor(deg[:, :, :], rowsum[:, :, :], least_sum[:, :, :], ALU.max).then_inc(sums_ready, 1)
                dve.wait_ge(sums_ready, g * 2 + 2)
                dve.reciprocal(deg_r[:, :, :], deg[:, :, :]).then_inc(factor_ready, 1)
                dve.wait_ge(factor_ready, g * 2 + 1)
                dve.tensor_tensor(factor[:, :, :], deg_r[:, :, :], w_pair[:, :, :],
                                  ALU.mult).then_inc(factor_ready, 1)

            def combine(g):
                dve.wait_ge(factor_ready, g * 2 + 2)
                dve.tensor_tensor(att_s[:, :, :, :].rearrange("p t w m -> p (t w) m"),
                                  att[:, :, :, :].rearrange("p t w m -> p (t w) m"),
                                  factor[:, :, :].rearrange("p t (w m) -> p (t w) m", m=1)
                                  .to_broadcast([P, 2 * TILES, N]), ALU.mult).then_inc(scaled_ready, 1)
                dve.wait_ge(scaled_ready, g + 1)
                for a in range(2):
                    rows = slice(a * N, (a + 1) * N)
                    dve.tensor_tensor(own(kmat, a, slice(0, TILES)), att_s[rows, :, LANG, :],
                                      att_s[rows, :, GRAV, :], ALU.add).then_inc(k_ready, 1)

            def kT_lo_part(g):
                dve.wait_ge(kT_hi_ready, g + 1)
                dve.tensor_tensor(kT_lo[:, :, :], trans[:, :, :], kT_hi[:, :, :].bitcast(F32),
                                  ALU.subtract).then_inc(kT_lo_ready, 1)

            def residual_tile(job, off, t, par):
                dve.wait_ge(ring_filled, job + (off + t + 1))
                dve.tensor_tensor(res[par][:, t, :], ring[(off + t) % RING][:, :], xs[par][:, t, :],
                                  ALU.add).then_inc(ring_drained, 1)

            def statistics_tile(job, off, t, par):
                dve.wait_ge(ring_drained, job + (off + t + 1))
                dve.bn_stats(stats[:, t, :], res[par][:, t, :]).then_inc(stats_ready, 1)

            def aggregate_tile(t):
                dve.bn_aggr(moments[:, t, :], stats[:, t, :]).then_inc(moments_ready, 1)

            def normalise_tile(t):
                dve.wait_ge(rstd_ready, GROUPS + t)
                dve.tensor_scalar(res[1][:, t, :], res[1][:, t, :], moments[:, t, 0:1], rstd_last[:, t:t + 1],
                                  ALU.subtract, ALU.mult).then_inc(last_ready, 1)

            def v_los(base, off, tiles):
                for t in tiles:
                    lo(base + (ZJOBS + t + 1), v_lo[:, t, :], ring[(off + t) % RING][:, :], v_hi[:, t, :])

            def turn(g, par, post=True, ahead=True):
                job = first_job(g)
                base = first_hi(g)
                z_lo(base, 0)
                if post:
                    distances(g - 1)
                z_lo(base, 1)
                z_lo(base, 2)
                if post:
                    gravity(g - 1)
                z_lo(base, 3)
                if post:
                    combine(g - 1)
                for k in range(DC, ZJOBS):
                    z_lo(base, k)
                off = ZJOBS
                if post:
                    kT_lo_part(g - 1)
                    if ahead:
                        for t in range(TILES):
                            residual_tile(job, off, t, 1 - par)
                        for t in range(TILES):
                            statistics_tile(job, off, t, 1 - par)
                        dve.wait_ge(stats_ready, g * TILES)
                    off += OJOBS
                diagonals(g)
                if post and ahead:
                    for t in range(TILES):
                        aggregate_tile(t)
                squared_norms(g)
                if ahead:
                    v_los(base, off, (0,))
                    symmetric(g)
                    v_los(base, off, (1,))
                    columns(g)
                    v_los(base, off, (2, 3))
                    for c in range(DC):
                        lo(base + (ZJOBS + VJOBS + c + 1), hT_lo[1 - par][:, c, :], ring[(off + c) % RING][:, :],
                           hT_hi[1 - par][:, c, :])
                    if post:
                        dve.wait_ge(out_stored, g * (16 * TILES))
                else:
                    for t in (0, 1):
                        residual_tile(job, off - OJOBS, t, 1 - par)
                    columns(g)
                    symmetric(g)
                    distances(g)
                    for t in (2, 3):
                        residual_tile(job, off - OJOBS, t, 1 - par)
                    gravity(g)
                    combine(g)
                    v_los(base, off, (0, 1, 2))
                    kT_lo_part(g)
                    statistics_tile(job, off - OJOBS, 0, 1 - par)
                    v_los(base, off, (3,))
                    for t in (1, 2, 3):
                        statistics_tile(job, off - OJOBS, t, 1 - par)
                    dve.wait_ge(stats_ready, g * TILES)
                    for t in range(TILES):
                        aggregate_tile(t)

            dve.memset(hT_hi[1][:, 0, 0:2 * P].bitcast(F32), 0.0).then_inc(warm_up_ready, 1)
            for which in range(2):
                for e in range(DC):
                    dve.wait_ge(w_hi_ready, which * DC + e + 1)
                    dve.tensor_tensor(w_lo[which][:, e, :], w_rows[which][:, e, :],
                                      w_hi[which][:, e, :].bitcast(F32), ALU.subtract).then_inc(w_lo_ready, 1)
            dve.wait_ge(consts, 8)
            for a in range(2):
                dve.memset(own(same_graph, a).bitcast(F32), 1.0).then_inc(own_ready, 1)
                dve.tensor_copy(ident_own[a * N:(a + 1) * N, :], own(ident, a)).then_inc(own_ready, 1)

            dve.wait_ge(sigma_exp, 2)
            dve.tensor_scalar(scal[:, 4:5], scal[:, 2:3], 1.0, None, ALU.add).then_inc(scalars, 1)
            dve.tensor_tensor(scal[:, 6:7], scal[:, 3:4], scal[:, 3:4], ALU.mult).then_inc(scalars, 1)
            dve.wait_ge(scalars, 2)
            dve.reciprocal(scal[:, 5:6], scal[:, 4:5]).then_inc(scalars, 1)
            dve.reciprocal(scal[:, 8:9], scal[:, 6:7]).then_inc(scalars, 1)
            dve.wait_ge(scalars, 4)
            dve.tensor_scalar(scal[:, 7:8], scal[:, 8:9], -0.5, None, ALU.mult).then_inc(scalars, 1)
            dve.tensor_copy(w_pair[:, :, 0], scal[:, 5:6].to_broadcast([P, TILES])).then_inc(scalars, 1)
            dve.wait_ge(scalars, 6)
            dve.tensor_scalar(w_pair[:, :, 1], w_pair[:, :, 0], -1.0, 1.0, ALU.mult, ALU.add).then_inc(scalars, 1)
            dve.wait_ge(scalars, 7)
            dve.tensor_copy(exponent_scale[:, :], scal[:, 7:8].to_broadcast([P, TILES])).then_inc(scalars, 1)

            dve.wait_ge(consts, 10)

            def u_los(which):
                for i in range(DC):
                    bank = u_banks[which][i]
                    dve.wait_ge(hi_written, U_JOB[which] + i + 1)
                    d = dve.scalar_tensor_tensor(
                        out=u_lo[:, which, i, i * P:(i + 1) * P], in0=bank[:, i * P:(i + 1) * P], scalar=0.5,
                        in1=u_hi[:, which, i, i * P:(i + 1) * P].bitcast(F32), op0=ALU.mult, op1=ALU.subtract)
                    if i < DC - 1:
                        d = dve.tensor_tensor(u_lo[:, which, i, (i + 1) * P:], bank[:, (i + 1) * P:],
                                              u_hi[:, which, i, (i + 1) * P:].bitcast(F32), ALU.subtract)
                    d.then_inc(ring_drained, 1)

            u_los(LANG)
            for f in range(DC):
                lo(WOT_JOB + f + 1, woT_lo[:, f, :], ring[f][:, :], woT_hi[:, f, :])
            for e in range(DC):
                dve.wait_ge(w_hi_ready, 2 * DC + e + 1)
                dve.tensor_tensor(w_lo[2][:, e, :], w_rows[2][:, e, :], w_hi[2][:, e, :].bitcast(F32),
                                  ALU.subtract).then_inc(w_lo_ready, 1)
            for c in range(DC):
                lo(XT0_JOB + c + 1, hT_lo[0][:, c, :], ring[c][:, :], hT_hi[0][:, c, :])
            u_los(GRAV)
            for i in range(DC):
                lo(C_JOB + i + 1, c_lo[:, i, :], ring[i][:, :], c_hi[:, i, :])
            groups(dve, lambda g, par: turn(g, par, post=False), turn, lambda g, par: turn(g, par, ahead=False))
            last_job = GROUPS * JOBS + (AHEAD - TJOBS)
            for t in range(TILES + 2):
                if t < TILES:
                    residual_tile(last_job, 0, t, 1)
                if 1 <= t <= TILES:
                    statistics_tile(last_job, 0, t - 1, 1)
                if t >= 2:
                    dve.wait_ge(var_ready, (GROUPS - 1) * 2)
                    dve.wait_ge(stats_ready, (GROUPS - 1) * TILES + t - 1)
                    aggregate_tile(t - 2)
                if t >= 3:
                    normalise_tile(t - 3)
            normalise_tile(TILES - 1)


_INS = ['x', 'adj', 'L0_gnn_W_lang', 'L0_gnn_W_grav', 'L0_gnn_W_V', 'L0_gnn_W_O',
        'L0_gnn_gate_logit', 'L0_gnn_log_sigma']


def kernel(**inputs):
    import numpy as _np
    import concourse.bacc as _bacc
    from concourse import mybir as _mybir
    from concourse.bass_utils import run_bass_kernel_spmd as _run

    nc = _bacc.Bacc("TRN2", target_bir_lowering=False, num_devices=1)
    arrays, args = {}, []
    for name in _INS:
        a = _np.ascontiguousarray(inputs[name])
        if a.ndim == 0:
            a = a.reshape(1)
        arrays[f"in_{name}_dram"] = a
        args.append(nc.dram_tensor(f"in_{name}_dram", a.shape, _mybir.dt.from_np(a.dtype), kind="ExternalInput").ap())
    shape = inputs["x"].shape
    args.append(nc.dram_tensor("out_0_dram", shape, _mybir.dt.float32, kind="ExternalOutput").ap())
    adj_resnorm(nc, *args)
    r = _run(nc, [arrays], core_ids=[0])
    return r.results[0]["out_0_dram"]
```
